# Optimizing a Trainium2 kernel written in Bass

```python
import numpy as np
import jax
import jax.numpy as jnp

def _softmax(x, axis=-1):
    return jax.nn.softmax(x, axis=axis)

def _gelu(x):
    return jax.nn.gelu(x, approximate=True)

def _silu(x):
    return jax.nn.silu(x)

def _sigmoid(x):
    return jax.nn.sigmoid(x)

def _layernorm(x, axis=-1, eps=1e-05):
    m = jnp.mean(x, axis=axis, keepdims=True)
    v = jnp.var(x, axis=axis, keepdims=True)
    return (x - m) / jnp.sqrt(v + eps)

def _scatter_add(tgt, idx, src, axis=0):
    return tgt.at[idx].add(src)

def _segment_sum(src, seg, n):
    return jax.ops.segment_sum(src, seg, n)
kernel_name = 'mk_xattn_ffn_d1_seqx_r8_439370'

def setup_inputs(seed: int=0):
    np.random.seed(seed)
    _w = jnp.asarray

    def _rec_inputs():
        import jax
        import jax.numpy as jnp
        _rk = jax.random.key(seed)
        x = -0.0002928 + 1 * jax.random.normal(jax.random.fold_in(_rk, 1), (1, 1024, 128), jnp.float32)
        _lenS = 1024 - jax.random.randint(jax.random.fold_in(_rk, 7), (1,), 0, max(1, 1024 // 4) + 1, jnp.int32)
        _lenS2 = 6404 - jax.random.randint(jax.random.fold_in(_rk, 8), (1,), 0, max(1, 6404 // 4) + 1, jnp.int32)
        _ctx_1024P = jax.random.normal(jax.random.fold_in(_rk, 11), (1, 16, 128), jnp.float32)
        _ctx_1024c = jax.random.dirichlet(jax.random.fold_in(_rk, 511), 0.3 * jnp.ones((16,), jnp.float32), (1, 6404))
        _ctx_1024t = jnp.einsum('bsk,bkd->bsd', _ctx_1024c, _ctx_1024P)
        _ctx_1024t = _ctx_1024t * jax.lax.rsqrt(jnp.mean(jnp.square(_ctx_1024t)) + 1e-12) * 0.953939
        ctx_1024 = -1.39393e-06 + 0.999914 * (_ctx_1024t + 0.3 * jax.random.normal(jax.random.fold_in(_rk, 611), (1, 6404, 128), jnp.float32))
        _validS = jnp.arange(1024)[None, :] < _lenS[:, None]
        _validS2 = jnp.arange(6404)[None, :] < _lenS2[:, None]
        _causal = jnp.tril(jnp.ones((1024, 1024), dtype=bool))
        mask_BxSxS2_bk1 = jnp.broadcast_to(_validS2[:, None, :], (1, 1024, 6404))
        return (x, ctx_1024, mask_BxSxS2_bk1)
    x, ctx_1024, mask_BxSxS2_bk1 = _rec_inputs()

    def _L0_xattn_setup():
        import jax, jax.numpy as jnp
        import numpy as np
        B, S, D, H = (2, 256, 128, 16)
        HD = D // H

        def _split_heads(x):
            b, s, _ = x.shape
            return x.reshape(b, s, H, HD).transpose(0, 2, 1, 3)
        key = jax.random.key(seed)
        ks = jax.random.split(key, 12)
        scale = 1.0 / np.sqrt(D)
        inp = {'query': jax.random.normal(ks[0], (B, S, D), jnp.float32), 'key': jax.random.normal(ks[1], (B, S, D), jnp.float32), 'value': jax.random.normal(ks[2], (B, S, D), jnp.float32), 'mask': jnp.broadcast_to(jnp.triu(jnp.ones((S, S), jnp.bool_), k=1), (B, S, S)), 'Wq': jax.random.normal(ks[3], (D, D), jnp.float32) * scale, 'bq': jnp.zeros((D,), jnp.float32), 'Wk': jax.random.normal(ks[4], (D, D), jnp.float32) * scale, 'bk': jnp.zeros((D,), jnp.float32), 'Wv': jax.random.normal(ks[5], (D, D), jnp.float32) * scale, 'bv': jnp.zeros((D,), jnp.float32), 'Wo': jax.random.normal(ks[6], (D, D), jnp.float32) * scale, 'bo': jnp.zeros((D,), jnp.float32)}
        return inp
    _L0_xattn_all = _L0_xattn_setup()
    _L0_xattn_in = {k: v for k, v in _L0_xattn_all.items() if k in ('Wq', 'bq', 'Wk', 'bk', 'Wv', 'bv', 'Wo', 'bo')}
    del _L0_xattn_all

    def _L0_ffn_setup():
        import jax, jax.numpy as jnp
        import numpy as np
        NUM_EXPERTS = 8
        TOP_K = 2
        key = jax.random.key(seed)
        ks = jax.random.split(key, 6)
        B, S, D, F = (2, 256, 128, 512)
        E = NUM_EXPERTS
        sd = 1.0 / np.sqrt(D)
        sf = 1.0 / np.sqrt(F)
        return {'x': jax.random.normal(ks[0], (B, S, D), dtype=jnp.float32), 'gate_w': jax.random.normal(ks[1], (E, D), dtype=jnp.float32) * sd, 'w1': jax.random.uniform(ks[2], (F, E, D), dtype=jnp.float32, minval=-sd, maxval=sd), 'b1': jax.random.uniform(ks[3], (E, F), dtype=jnp.float32, minval=-sd, maxval=sd), 'w2': jax.random.uniform(ks[4], (D, E, F), dtype=jnp.float32, minval=-sf, maxval=sf), 'b2': jax.random.uniform(ks[5], (E, D), dtype=jnp.float32, minval=-sf, maxval=sf)}
    _L0_ffn_all = _L0_ffn_setup()
    _L0_ffn_in = {k: v for k, v in _L0_ffn_all.items() if k in ('gate_w', 'w1', 'b1', 'w2', 'b2')}
    del _L0_ffn_all
    return {'x': x, 'ctx_1024': ctx_1024, 'mask_BxSxS2_bk1': mask_BxSxS2_bk1, 'L0_xattn_Wq': _L0_xattn_in['Wq'], 'L0_xattn_bq': _L0_xattn_in['bq'], 'L0_xattn_Wk': _L0_xattn_in['Wk'], 'L0_xattn_bk': _L0_xattn_in['bk'], 'L0_xattn_Wv': _L0_xattn_in['Wv'], 'L0_xattn_bv': _L0_xattn_in['bv'], 'L0_xattn_Wo': _L0_xattn_in['Wo'], 'L0_xattn_bo': _L0_xattn_in['bo'], 'L0_ffn_gate_w': _L0_ffn_in['gate_w'], 'L0_ffn_w1': _L0_ffn_in['w1'], 'L0_ffn_b1': _L0_ffn_in['b1'], 'L0_ffn_w2': _L0_ffn_in['w2'], 'L0_ffn_b2': _L0_ffn_in['b2']}

def reference(x, ctx_1024, mask_BxSxS2_bk1, L0_xattn_Wq, L0_xattn_bq, L0_xattn_Wk, L0_xattn_bk, L0_xattn_Wv, L0_xattn_bv, L0_xattn_Wo, L0_xattn_bo, L0_ffn_gate_w, L0_ffn_w1, L0_ffn_b1, L0_ffn_w2, L0_ffn_b2):
    import jax
    import jax.numpy as jnp

    def _L0_xattn_ref(query, key, value, mask, Wq, bq, Wk, bk, Wv, bv, Wo, bo):
        import jax, jax.numpy as jnp
        import numpy as np
        B, S, D, H = (2, 256, 128, 16)
        HD = D // H

        def _split_heads(x):
            b, s, _ = x.shape
            return x.reshape(b, s, H, HD).transpose(0, 2, 1, 3)
        q = _split_heads(query @ Wq.T + bq)
        k = _split_heads(key @ Wk.T + bk)
        v = _split_heads(value @ Wv.T + bv)
        scores = jnp.einsum('bhqd,bhkd->bhqk', q, k) / jnp.sqrt(jnp.float32(HD))
        scores = jnp.where(mask[:, None, :, :], jnp.finfo(scores.dtype).min, scores)
        attn = jax.nn.softmax(scores, axis=-1)
        ctx = jnp.einsum('bhqk,bhkd->bhqd', attn, v)
        merged = ctx.transpose(0, 2, 1, 3).reshape(query.shape[0], -1, D)
        out = merged @ Wo.T + bo
        return out

    def _L0_ffn_ref(x, gate_w, w1, b1, w2, b2):
        import jax, jax.numpy as jnp
        import numpy as np
        NUM_EXPERTS = 8
        TOP_K = 2
        logits = jnp.einsum('bsd,ed->bse', x, gate_w)
        probs = jax.nn.softmax(logits, axis=-1)
        topk_probs, topk_idx = jax.lax.top_k(probs, TOP_K)
        oh = jax.nn.one_hot(topk_idx, NUM_EXPERTS, dtype=x.dtype)
        h = jnp.einsum('bsd,fed,bske->bskf', x, w1, oh)
        h = h + jnp.take(b1, topk_idx, axis=0)
        h = jax.nn.gelu(h)
        y = jnp.einsum('bskf,def,bske->bskd', h, w2, oh)
        y = y + jnp.take(b2, topk_idx, axis=0)
        out = jnp.sum(y * topk_probs[..., None], axis=-2)
        return out
    x = x + _L0_xattn_ref(_layernorm(x, axis=-1), ctx_1024, ctx_1024, mask_BxSxS2_bk1, L0_xattn_Wq, L0_xattn_bq, L0_xattn_Wk, L0_xattn_bk, L0_xattn_Wv, L0_xattn_bv, L0_xattn_Wo, L0_xattn_bo)
    x = x + _L0_ffn_ref(_layernorm(x, axis=-1), L0_ffn_gate_w, L0_ffn_w1, L0_ffn_b1, L0_ffn_w2, L0_ffn_b2)
    return x

_drawn_inputs = setup_inputs


def setup_inputs(seed=0):
    import zlib

    import numpy as np

    out = dict(_drawn_inputs(seed))
    spreads = {'L0_xattn_bq': (0.0, 0.355),
     'L0_xattn_bk': (0.0, 0.8),
     'L0_xattn_bv': (0.0, 0.1),
     'L0_xattn_bo': (0.0, 0.1)}
    factors = {'L0_ffn_b1': 7.297, 'L0_ffn_b2': 5.16}
    for name, (base, spread) in spreads.items():
        noise = np.random.default_rng([zlib.crc32(name.encode()), seed]).standard_normal(out[name].shape)
        drawn = base * np.exp(spread * noise) if base else spread * noise
        out[name] = jnp.asarray(drawn.astype(out[name].dtype))
    for name, factor in factors.items():
        out[name] = (out[name] * factor).astype(out[name].dtype)
    return out
```

```python
import concourse.bass as bass
from concourse import mybir
from contextlib import ExitStack

F32 = mybir.dt.float32
BF16 = mybir.dt.bfloat16
U8 = mybir.dt.uint8
U16 = mybir.dt.uint16
I32 = mybir.dt.int32
ACT = mybir.ActivationFunctionType
ALU = mybir.AluOpType
AX = mybir.AxisListType

P = 128
S, D, H = 1024, 128, 16
HD = D // H
S2 = 6404
E, F = 8, 512
QT = S // P
FT = F // P
T = -(-S2 // P)
PAD = T * P - S2
KW = T * P
SCALE = float(HD) ** -0.5
BIG = 2.0 ** 100
EPS = 1e-5
GATE_STEPS = 18
NC = 9
SHIFT_ROW = 96


def build(nc, x, ctx_in, mask, Wq, bq, Wk, bk, Wv, bv, Wo, bo, gate_w, w1, b1, w2, b2, out):
    with ExitStack() as es:
        def sb(name, shape, dt):
            return es.enter_context(nc.sbuf_tensor(name, shape, dt))

        def sem(name):
            return es.enter_context(nc.semaphore(name))

        kparts_dram = nc.dram_tensor("kparts_dram", (3, P, P), BF16, kind="Internal").ap()
        qparts_dram = nc.dram_tensor("qparts_dram", (3, P, S), BF16, kind="Internal").ap()

        mask_u8 = sb("mask_u8", [P, QT, KW], U8)
        ctx_sb = sb("ctx_sb", [P, T, D], F32)
        x_sb = sb("x_sb", [P, QT, D], F32)
        arenaA = sb("arenaA", [P, 4096], F32)
        arenaB = sb("arenaB", [P, 4, 1024], F32)
        qS = sb("qS", [P, H, S], BF16)
        arenaC = sb("arenaC", [P, 1664], F32)
        wT = sb("wT", [P, 4, D], F32)
        gateT = sb("gateT", [P, E], F32)
        b1T = sb("b1T", [P, FT, E], F32)
        b2_sb = sb("b2_sb", [E, D], F32)
        w1T = sb("w1T", [P, E, FT, P], F32)
        w2T = sb("w2T", [P, E, FT, D], F32)
        brow = sb("brow", [1, 4, D], F32)
        ones = sb("ones", [P, 512], F32)
        ident = sb("ident", [P, P], F32)
        identb = sb("identb", [P, P], BF16)
        nbig = sb("nbig", [P, P], BF16)
        maskT = sb("maskT", [P, 2, S], BF16)
        stat = sb("stat", [P, 6, QT], F32)
        cbuf = sb("cbuf", [P, D], F32)
        cT = sb("cT", [P, P], F32)
        kres = sb("kres", [P, 2, P], F32)
        kparts = sb("kparts", [P, 3, P], BF16)
        knext = sb("knext", [P, H, P], BF16)
        vcur = sb("vcur", [P, H, 32], F32)
        cnt4 = sb("cnt4", [P, T], F32)
        tcol = sb("tcol", [64, 4], F32)
        tri = sb("tri", [64, 64], F32)
        iota_s = sb("iota_s", [64, 64], F32)
        iota_p = sb("iota_p", [64, 1], F32)
        hot = sb("hot", [64, 64], F32)
        plan = sb("plan", [1, 72], I32)
        s2row = sb("s2row", [1, P], F32)
        csum = sb("csum", [P, D], F32)
        csT = sb("csT", [P, 1], F32)
        vsrow = sb("vsrow", [1, D], F32)
        vsumB = sb("vsumB", [P, D], F32)
        g1 = sb("g1", [P, 6, QT], F32)
        iota_e = sb("iota_e", [P, QT * E], F32)

        peak = maskT[:, :, :].rearrange("p a q -> p (a q)").bitcast(F32)
        tmax = peak[:, 0:128].rearrange("p (h t) -> p h t", t=QT)
        rmax = peak[:, 768:896].rearrange("p (h t) -> p h t", t=QT)
        mres = peak[:, 128:384].rearrange("p (a k) -> p a k", a=2)
        mparts = peak[:, 384:576].bitcast(BF16).rearrange("p (c k) -> p c k", c=3)
        mpT = peak[:, 576:768].bitcast(BF16).rearrange("p (c k) -> p c k", c=3)

        xn = arenaA[:, 0:1024].rearrange("p (t d) -> p t d", d=D)
        sq = arenaA[:, 1024:2048].rearrange("p (t d) -> p t d", d=D)
        qres = [arenaA[:, 1024:2048]]
        qparts = arenaA[:, 2048:3584].bitcast(BF16).rearrange("p (c q) -> p c q", c=3)
        early = w2T[:, :, :, :].rearrange("p e a d -> p (e a d)")
        xT = early[:, 0:1024]
        wraw = early[:, 1024:1536].rearrange("p (a d) -> p a d", a=4)
        gate_raw = early[0:E, 1536:1664]
        b1_raw = early[0:E, 1664:2176]
        and_acc = arenaC[:, 0:KW // 4].bitcast(I32)
        kcur = arenaC[:, 0:1024].bitcast(BF16).rearrange("p (h k) -> p h k", h=H)
        mbf = arenaC[:, 1024:1536].bitcast(BF16).rearrange("p (t k) -> p t k", t=QT)
        w2raw = arenaA[:, :].rearrange("p (e f) -> p e f", e=E)
        accU = arenaA[:, :].rearrange("p (g q) -> p g q", g=4)
        w1raw = arenaB[:, :, :].rearrange("p a (e d) -> p a e d", e=E)
        after = ctx_sb[:, :, :].rearrange("p t d -> p (t d)")
        x2 = after[:, 0:1024].rearrange("p (t d) -> p t d", d=D)
        xn2 = after[:, 1024:2048].rearrange("p (t d) -> p t d", d=D)
        x2T = after[:, 2048:3072]
        ctxq = after[:, 3072:4096].rearrange("p (t d) -> p t d", d=D)
        ctxqT = after[:, 4096:5120]
        sq2 = after[:, 5120:6144].rearrange("p (t d) -> p t d", d=D)
        g = after[:, 5120:5888].rearrange("p (a b) -> p a b", a=12)
        epi_e = after[0:E, 3072:4096]
        hT = mask_u8[:, :, :].rearrange("p t k -> p (t k)").bitcast(F32)[:, 0:8192].rearrange(
            "p (b t q) -> p b t q", b=2, t=FT)
        maskw = mask_u8[:, :, :].bitcast(I32)

        bank = es.enter_context(nc.psum_tensor("bank", [P, 8, 512], F32))
        maskT_ps = bank[:, 7, :].bitcast(BF16)
        b6 = bank[:, 6, :]

        names = ("x_in w_in row_in gate_in b1_in b2_in w1_in w2_in ctx_in ctxpad mask_in pad const ln "
                 "sqrt xnT_ps xT_sb q_ps q_sb qw qr qzero wt_ps wt_sb wtb_ps wtb_sb "
                 "and_ cs cs_ps cs_sb pl_ps pl_sb plan_ready act_ev pe_w acc0 "
                 "m_cb m_ct m_ctsb m_kv m_kch m_kw m_kr m_kc m_mb m_qk m_red m_max m_fin m_finT m_finsb shift "
                 "cb ct ctsb kv kch kw kr kc vc mb mt mc qk ex pv ac "
                 "u_ps u_dve cq_ps cq_sb at_ps x2s ln2 sqrt2 x2T_ps x2T_sb lg gt gtexp gT_ps gT_sb "
                 "hps hact yps yacc b2ps moe outs kinit vinit fin_x sp_at pool_at").split()
        s = {n: sem(n) for n in names}
        mask_in = [sem(f"mask_in{t}") for t in range(QT)]

        block = es.enter_context(nc.Block())

        @block.sync
        def _(sp):
            sp.dma_start(x_sb[:, :, :], x.rearrange("a (p t) d -> p (a t) d", t=QT)).then_inc(s["x_in"], 16)
            for i, w in enumerate((Wq, Wk, Wv, Wo)):
                sp.dma_start(wraw[:, i, :], w).then_inc(s["w_in"], 16)
            for i, b in enumerate((bq, bk, bv, bo)):
                sp.dma_start(brow[0:1, i, :], b.rearrange("(a n) -> a n", a=1)).then_inc(s["row_in"], 16)
            m = mask.rearrange("a (p t) k -> p (a t) k", t=QT)
            for t in range(QT):
                sp.dma_start(mask_u8[:, t, PAD:KW], m[:, t, :]).then_inc(mask_in[t], 16)
            sp.wait_ge(s["q_sb"], 4)
            sp.dma_start(qparts_dram.rearrange("c p q -> p c q"), qparts[:, :, :]).then_inc(s["qw"], 16)
            sp.wait_ge(s["qw"], 16)
            sp.wait_ge(s["qzero"], 1)
            for c in range(NC):
                sp.dma_start(qS[c * HD:(c + 1) * HD, :, :],
                             qparts_dram[c // 3, :, :].rearrange("(h d) q -> d h q", d=HD)).then_inc(s["qr"], 16)

            def key_rows(i, chain, written, read, copied):
                sp.wait_ge(chain, i * 4 + 4)
                sp.dma_start(kparts_dram.rearrange("c p k -> p c k"), kparts[:, :, :]).then_inc(written, 16)
                sp.wait_ge(written, i * 16 + 16)
                sp.sem_inc(s["sp_at"], 1)
                sp.wait_ge(copied, i + 1)
                for c in range(NC):
                    sp.dma_start(knext[c * HD:(c + 1) * HD, :, :],
                                 kparts_dram[c % 3, :, :].rearrange("(h d) k -> d h k", d=HD)).then_inc(read, 16)

            sp.wait_ge(s["plan_ready"], 1)
            n = sp.value_load(plan[0:1, 64:65], min_val=1, max_val=T)
            sp.wait_ge(s["kinit"], 1)
            with sp.Fori(0, n + 1) as i:
                key_rows(i, s["m_kch"], s["m_kw"], s["m_kr"], s["m_kc"])
            sp.wait_ge(s["m_kr"], n * 144 + 144)
            sp.sem_inc(s["sp_at"], 1)
            for c in range(3):
                sp.wait_ge(s["m_finsb"], 1)
                sp.dma_start(qS[SHIFT_ROW + c:SHIFT_ROW + c + 1, :, :].rearrange("a h (t q) -> a (h t) q", q=P),
                             mpT[:, c, :]).then_inc(s["shift"], 16)
            with sp.Fori(0, n + 1) as i:
                key_rows(i, s["kch"], s["kw"], s["kr"], s["kc"])
            sp.wait_ge(s["yacc"], E * QT + 1)
            sp.dma_start(out.rearrange("a (p t) d -> p (a t) d", t=QT), x2).then_inc(s["outs"], 16)
            sp.wait_ge(s["outs"], 16)

        @block.gpsimd
        def _(pool):
            pool.dma_start(ctx_sb[:, 1:T, :], ctx_in[0, S2 - (T - 1) * P:S2, :].rearrange("(t p) d -> p t d", p=P)
                           ).then_inc(s["ctx_in"], 16)
            pool.dma_start(w1raw, w1.rearrange("(a p) e d -> p a e d", p=P)).then_inc(s["w1_in"], 16)
            pool.dma_start(gate_raw[:, :], gate_w).then_inc(s["gate_in"], 16)
            pool.dma_start(b1_raw[:, :], b1).then_inc(s["b1_in"], 16)
            pool.dma_start(b2_sb[:, :], b2).then_inc(s["b2_in"], 16)
            nc.gpsimd.memset(ident[:, :], 0.0).then_inc(s["const"], 1)
            pool.wait_ge(s["const"], 1)
            nc.gpsimd.affine_select(out=ident[:, :], in_=ident[:, :], compare_op=ALU.not_equal, fill=1.0,
                                    base=0, pattern=[[-1, P]], channel_multiplier=1).then_inc(s["const"], 1)
            nc.gpsimd.memset(ones[:, :], 1.0).then_inc(s["const"], 1)
            nc.gpsimd.memset(s2row[:, :], float(S2)).then_inc(s["const"], 1)
            pool.wait_ge(s["const"], 4)
            nc.gpsimd.tensor_copy(identb[:, :], ident[:, :]).then_inc(s["const"], 1)
            nc.gpsimd.memset(nbig[:, :], 0.0).then_inc(s["const"], 1)
            nc.gpsimd.memset(tri[:, :], 1.0).then_inc(s["const"], 1)
            pool.wait_ge(s["const"], 7)
            nc.gpsimd.affine_select(out=nbig[:, :], in_=nbig[:, :], compare_op=ALU.not_equal, fill=-BIG,
                                    base=0, pattern=[[-1, P]], channel_multiplier=1).then_inc(s["const"], 1)
            nc.gpsimd.affine_select(out=tri[:, :], in_=tri[:, :], compare_op=ALU.is_gt, fill=0.0,
                                    base=0, pattern=[[1, 64]], channel_multiplier=-1).then_inc(s["const"], 1)
            nc.gpsimd.iota(iota_s[:, :], [[1, 64]], base=0, channel_multiplier=0,
                           allow_small_or_imprecise_dtypes=True).then_inc(s["const"], 1)
            nc.gpsimd.iota(iota_p[:, :], [[0, 1]], base=0, channel_multiplier=1,
                           allow_small_or_imprecise_dtypes=True).then_inc(s["const"], 1)
            nc.gpsimd.iota(iota_e[:, :], [[0, QT], [1, E]], base=0, channel_multiplier=0,
                           allow_small_or_imprecise_dtypes=True).then_inc(s["const"], 1)
            nc.gpsimd.memset(mask_u8[:, :, 0:PAD], 1).then_inc(s["pad"], 1)
            nc.gpsimd.memset(ctx_sb[:, 0, :], 0.0).then_inc(s["ctxpad"], 1)
            pool.wait_ge(s["ctxpad"], 1)
            pool.dma_start(ctx_sb[PAD:P, 0, :], ctx_in[0, 0:P - PAD, :]).then_inc(s["ctx_in"], 16)
            nc.gpsimd.memset(qS[64:P, :, :].bitcast(F32), 0.0).then_inc(s["qzero"], 1)
            pool.wait_ge(s["qzero"], 1)
            nc.gpsimd.memset(knext[64:P, :, :].bitcast(F32), 0.0).then_inc(s["qzero"], 1)
            pool.wait_ge(s["qzero"], 2)
            nc.gpsimd.memset(knext[SHIFT_ROW:SHIFT_ROW + 3, :, :], 1.0).then_inc(s["kinit"], 1)
            pool.wait_ge(s["kinit"], 1)
            nc.gpsimd.memset(vcur[:, :, :], 0.0).then_inc(s["qzero"], 1)
            pool.wait_ge(s["qzero"], 3)
            nc.gpsimd.memset(vcur[:, :, HD:HD + 1], 1.0).then_inc(s["vinit"], 1)
            pool.wait_ge(s["wtb_sb"], 8)
            pool.wait_ge(s["qw"], 16)
            pool.dma_start(w2raw, w2.rearrange("d e f -> d e f")).then_inc(s["w2_in"], 16)

            pool.wait_ge(s["plan_ready"], 1)
            pool.wait_ge(s["ctx_in"], 32)
            n = pool.value_load(plan[0:1, 64:65], min_val=1, max_val=T)

            def tile_in(i, cb, ct, mb, mask_used, per_tile):
                tile = pool.value_load(plan[0:1, bass.ds(i, 1)], min_val=0, max_val=T - 1)
                pool.wait_ge(ct, i + 1)
                nc.gpsimd.tensor_copy(cbuf[:, :], ctx_sb[:, bass.ds(tile, 1), :].rearrange("p a d -> p (a d)")).then_inc(cb, 1)
                pool.wait_ge(mask_used, i * per_tile + 1)
                nc.gpsimd.tensor_copy(mbf[:, :, :], mask_u8[:, :, bass.ds(tile * P, P)]).then_inc(mb, 1)

            with pool.Fori(0, n + 1) as i:
                tile_in(i, s["m_cb"], s["m_ct"], s["m_mb"], s["m_qk"], 16)
            pool.wait_ge(s["m_ct"], n + 2)
            pool.sem_inc(s["pool_at"], 1)
            pool.wait_ge(s["m_mb"], n + 1)
            pool.sem_inc(s["pool_at"], 1)
            with pool.Fori(0, n + 1) as i:
                tile_in(i, s["cb"], s["ct"], s["mb"], s["mt"], 1)

        def layer_norm(dve, xin, xout, scratch, done, sqrt_done):
            c = [0]

            def step(ins):
                c[0] += 1
                ins.then_inc(done, 1)
                dve.wait_ge(done, c[0])

            mean, var, root, inv, t1 = (stat[:, k, :] for k in range(5))
            step(nc.vector.tensor_reduce(mean, xin, axis=AX.X, op=ALU.add))
            step(nc.vector.tensor_scalar(mean, mean, 1.0 / D, None, ALU.mult))
            step(nc.vector.tensor_tensor(xout, xin, mean.rearrange("p (t a) -> p t a", a=1).broadcast_to([P, QT, D]), ALU.subtract))
            step(nc.vector.tensor_tensor(scratch, xout, xout, ALU.mult))
            step(nc.vector.tensor_reduce(var, scratch, axis=AX.X, op=ALU.add))
            step(nc.vector.tensor_scalar(var, var, 1.0 / D, EPS, ALU.mult, ALU.add))
            dve.wait_ge(sqrt_done, 1)
            step(nc.vector.reciprocal(inv, root))
            step(nc.vector.tensor_tensor(t1, var, inv, ALU.mult))
            step(nc.vector.tensor_tensor(t1, t1, root, ALU.add))
            step(nc.vector.tensor_scalar(t1, t1, 0.5, None, ALU.mult))
            step(nc.vector.reciprocal(inv, t1))
            nc.vector.tensor_tensor(xout, xout, inv.rearrange("p (t a) -> p t a", a=1).broadcast_to([P, QT, D]), ALU.mult).then_inc(done, 1)

        def parts3(dve, dst, src, res, chain, base):
            nc.vector.tensor_copy(dst[0], src).then_inc(chain, 1)
            dve.wait_ge(chain, base + 1)
            nc.vector.tensor_tensor(res[0], src, dst[0], ALU.subtract).then_inc(chain, 1)
            dve.wait_ge(chain, base + 2)
            nc.vector.tensor_copy(dst[1], res[0]).then_inc(chain, 1)
            dve.wait_ge(chain, base + 3)
            nc.vector.tensor_tensor(dst[2], res[0], dst[1], ALU.subtract).then_inc(chain, 1)

        @block.vector
        def _(dve):
            dve.wait_ge(s["x_in"], 16)
            layer_norm(dve, x_sb[:, :, :], xn, sq, s["ln"], s["sqrt"])
            for k in range(2):
                dve.wait_ge(s["xnT_ps"], k + 1)
                nc.vector.tensor_copy(xT[:, 512 * k:512 * k + 512], bank[:, k, :]).then_inc(s["xT_sb"], 1)
            dve.wait_ge(s["q_ps"], 1)
            qp = bank[:, 2:4, :].rearrange("p a b -> p (a b)")
            parts3(dve, [qparts[:, k, :] for k in range(3)], qp, [qres[0]], s["q_sb"], 0)

            dve.wait_ge(s["pad"], 1)
            dve.wait_ge(mask_in[0], 16)
            for t in range(1, QT):
                dve.wait_ge(mask_in[t], 16)
                if t > 1:
                    dve.wait_ge(s["and_"], t - 1)
                nc.vector.tensor_tensor(and_acc[:, :], maskw[:, 0, :] if t == 1 else and_acc[:, :], maskw[:, t, :],
                                        ALU.bitwise_and).then_inc(s["and_"], 1)
            c = QT - 1
            w = P // 4
            av = and_acc[:, :].rearrange("p (t w) -> p t w", w=w)
            while w > 1:
                w //= 2
                dve.wait_ge(s["and_"], c)
                nc.vector.tensor_tensor(av[:, :, 0:w], av[:, :, 0:w], av[:, :, w:2 * w], ALU.bitwise_and).then_inc(s["and_"], 1)
                c += 1
            dve.wait_ge(s["and_"], c)
            ab = and_acc[:, :].bitcast(U8).rearrange("p (t b) -> p t b", b=P)[:, :, 0:4]
            nc.vector.tensor_reduce(cnt4[:, :], ab, axis=AX.X, op=ALU.add).then_inc(s["pl_sb"], 1)
            dve.wait_ge(s["pl_ps"], 1)
            nc.vector.tensor_scalar(tcol[0:T, 0:1], b6[0:T, 0:1], 4.0 * P - 0.5, None, ALU.is_lt).then_inc(s["pl_sb"], 1)
            dve.wait_ge(s["pl_ps"], 2)
            nc.vector.tensor_copy(tcol[0:T, 1:2], b6[0:T, 1:2]).then_inc(s["pl_sb"], 1)
            dve.wait_ge(s["pl_sb"], 3)
            nc.vector.tensor_scalar(hot[0:T, :], iota_s[0:T, :], tcol[0:T, 1:2], tcol[0:T, 0:1], ALU.is_equal, ALU.mult).then_inc(s["pl_sb"], 1)
            dve.wait_ge(s["pl_ps"], 3)
            nc.vector.tensor_copy(plan[0:1, 0:64], b6[0:1, 64:128]).then_inc(s["pl_sb"], 1)
            nc.vector.tensor_scalar(plan[0:1, 64:65], b6[0:1, 128:129], 1.0, None, ALU.max).then_inc(s["plan_ready"], 1)

            dve.wait_ge(s["ctx_in"], 32)
            nc.vector.tensor_reduce(csum[:, :], ctx_sb[:, :, :].rearrange("p t d -> p d t"), axis=AX.X, op=ALU.add).then_inc(s["cs_sb"], 1)
            dve.wait_ge(s["cs_ps"], 1)
            nc.vector.tensor_copy(csT[:, :], b6[:, 200:201]).then_inc(s["cs_sb"], 1)
            dve.wait_ge(s["cs_ps"], 2)
            nc.vector.tensor_copy(vsrow[:, :], b6[0:1, 256:384]).then_inc(s["cs_sb"], 1)
            dve.wait_ge(s["cs_ps"], 3)
            nc.vector.tensor_copy(vsumB[:, :], b6[:, 384:512]).then_inc(s["cs_sb"], 1)

            dve.wait_ge(s["plan_ready"], 1)
            n = dve.value_load(plan[0:1, 64:65], min_val=1, max_val=T)
            nc.vector.memset(rmax[:, :, :], -4.0 * BIG).then_inc(s["m_max"], 1)

            def key_parts(i, ct, ctsb, kv, kch):
                dve.wait_ge(ct, i + 2)
                nc.vector.tensor_copy(cT[:, :], b6[:, 0:P]).then_inc(ctsb, 1)
                dve.wait_ge(kv, i + 1)
                parts3(dve, [kparts[:, k, :] for k in range(3)], b6[:, P:2 * P], [kres[:, 0, :]], kch, i * 4)

            dve.sem_inc(s["m_kc"], 1)
            dve.sem_inc(s["m_red"], 2)

            def key_parts_max(i):
                key_parts(i, s["m_ct"], s["m_ctsb"], s["m_kv"], s["m_kch"])

            key_parts_max(0)
            with dve.Fori(0, n) as i:
                dve.wait_ge(s["m_kr"], i * 144 + 144)
                dve.wait_ge(s["m_qk"], i * 16 + 1)
                nc.vector.tensor_copy(kcur[:, :, :], knext[:, :, :]).then_inc(s["m_kc"], 1)
                for u in range(16):
                    t, hh = u // 2, u % 2
                    dve.wait_ge(s["m_qk"], i * 16 + u + 2)
                    if u == 0:
                        dve.wait_ge(s["m_max"], i + 1)
                    nc.vector.tensor_reduce(tmax[:, 8 * hh:8 * hh + 8, t], bank[:, 2 * hh:2 * hh + 2, :].rearrange("p a (h k) -> p (a h) k", k=P),
                                            axis=AX.X, op=ALU.max).then_inc(s["m_red"], 1)
                    if u == 3:
                        dve.wait_ge(s["m_kw"], i * 16 + 16)
                        key_parts_max(i + 1)
                dve.wait_ge(s["m_red"], i * 16 + 18)
                nc.vector.tensor_tensor(rmax[:, :, :], rmax[:, :, :], tmax[:, :, :], ALU.max).then_inc(s["m_max"], 1)
            dve.wait_ge(s["m_max"], n + 1)
            m2 = rmax[:, :, :].rearrange("p h t -> p (h t)")
            nc.vector.tensor_scalar(mres[:, 0, :], m2, -BIG / 4, -1.0, ALU.max, ALU.mult).then_inc(s["m_fin"], 1)
            dve.wait_ge(s["m_fin"], 1)
            parts3(dve, [mparts[:, k, :] for k in range(3)], mres[:, 0, :], [mres[:, 1, :]], s["m_fin"], 1)
            dve.wait_ge(s["m_finT"], 1)
            nc.vector.tensor_copy(mpT[:, :, :], bank[:, 0, 0:192].bitcast(BF16).rearrange("p (c q) -> p c q", c=3)).then_inc(s["m_finsb"], 1)
            dve.wait_ge(s["m_kr"], n * 144 + 144)
            dve.wait_ge(s["shift"], 48)

            dve.wait_ge(s["wtb_ps"], 16)
            nc.vector.memset(arenaA[:, :], 0.0).then_inc(s["ac"], 1)
            dve.sem_inc(s["kc"], 1)

            def parts(i):
                key_parts(i, s["ct"], s["ctsb"], s["kv"], s["kch"])

            def key_copy(i):
                dve.wait_ge(s["kr"], i * 144 + 144)
                nc.vector.tensor_copy(kcur[:, :, :], knext[:, :, :]).then_inc(s["kc"], 1)

            def mask_copy(i):
                dve.wait_ge(s["mt"], i + 2)
                nc.vector.tensor_copy(maskT[:, bass.ds(i % 2, 1), :], maskT_ps.rearrange("p (a q) -> p a q", a=1)).then_inc(s["mc"], 1)

            def value_copy():
                nc.vector.tensor_copy(vcur[:, :, 0:HD], b6[:, 2 * P:3 * P].rearrange("p (h d) -> p h d", d=HD)).then_inc(s["vc"], 1)

            def add(i, k):
                dve.wait_ge(s["pv"], i * 8 + k + 3)
                dve.wait_ge(s["ac"], i * 8 + k + 2)
                a = accU[:, k // 2, 512 * (k % 2):512 * (k % 2) + 512]
                nc.vector.tensor_tensor(a, bank[:, 4 + k % 2, :], a, ALU.add).then_inc(s["ac"], 1)

            dve.sem_inc(s["ac"], 1)
            dve.wait_ge(s["m_kw"], n * 16 + 16)
            parts(0)
            key_copy(0)
            dve.wait_ge(s["vinit"], 1)
            value_copy()
            mask_copy(0)
            with dve.Fori(0, n) as i:
                for k in range(8):
                    if k >= 1:
                        add(i, k - 1)
                    if k == 2:
                        dve.wait_ge(s["kw"], i * 16 + 16)
                        parts(i + 1)
                        mask_copy(i + 1)
                    if k == 6:
                        dve.wait_ge(s["qk"], i * 16 + 16)
                        key_copy(i + 1)
                add(i, 7)
                value_copy()
            dve.wait_ge(s["ac"], n * 8 + 2)
            nc.vector.memset(stat[:, 5, :], 0.0).then_inc(s["fin_x"], 1)

            for hf in range(2):
                dve.wait_ge(s["u_ps"], hf + 1)
                U = bank[:, 4 * hf:4 * hf + 4, :].rearrange("p t (k c) -> p (t k) c", c=32)
                c0 = 5 * hf
                flag, weight, inv, tmp = (arenaB[:, 2 + (k == 3), 64 * (k % 3):64 * (k % 3) + (512 if k == 3 else 64)] for k in range(4))
                cq = ctxq[:, 4 * hf:4 * hf + 4, :].rearrange("p t (h c) -> p (t h) c", c=HD)
                tmp = tmp.rearrange("p (k c) -> p k c", c=HD)
                over = lambda a: a.rearrange("p (k a) -> p k a", a=1).broadcast_to([P, 64, HD])
                if hf:
                    dve.wait_ge(s["u_dve"], 5)
                nc.vector.tensor_scalar(flag, U[:, :, HD], 0.0, None, ALU.is_equal).then_inc(s["u_dve"], 1)
                dve.wait_ge(s["u_dve"], c0 + 1)
                nc.vector.scalar_tensor_tensor(weight, flag, float(S2), U[:, :, HD], ALU.mult, ALU.add).then_inc(s["u_dve"], 1)
                for t in range(4):
                    last = nc.vector.tensor_tensor(tmp[:, H * t:H * t + H, :], over(flag)[:, H * t:H * t + H, :],
                                                   vsumB[:, :].rearrange("p (h c) -> p h c", c=HD), ALU.mult)
                last.then_inc(s["u_dve"], 1)
                dve.wait_ge(s["u_dve"], c0 + 3)
                nc.vector.tensor_tensor(cq, tmp, U[:, :, 0:HD], ALU.add)
                nc.vector.reciprocal(inv, weight).then_inc(s["u_dve"], 1)
                dve.wait_ge(s["u_dve"], c0 + 4)
                nc.vector.tensor_tensor(cq, cq, over(inv), ALU.mult).then_inc(s["u_dve"], 1)
            for k in range(2):
                dve.wait_ge(s["cq_ps"], k + 1)
                nc.vector.tensor_copy(ctxqT[:, 512 * k:512 * k + 512], bank[:, k, :]).then_inc(s["cq_sb"], 1)
            dve.wait_ge(s["at_ps"], 1)
            nc.vector.tensor_tensor(x2, x_sb[:, :, :], bank[:, 2:4, :].rearrange("p a (t d) -> p (a t) d", d=D), ALU.add).then_inc(s["x2s"], 1)
            dve.wait_ge(s["x2s"], 1)
            layer_norm(dve, x2, xn2, sq2, s["ln2"], s["sqrt2"])
            for k in range(2):
                dve.wait_ge(s["x2T_ps"], k + 1)
                nc.vector.tensor_copy(x2T[:, 512 * k:512 * k + 512], bank[:, k, :]).then_inc(s["x2T_sb"], 1)

            c = [0]

            def step(ins):
                c[0] += 1
                ins.then_inc(s["gt"], 1)
                dve.wait_ge(s["gt"], c[0])

            dve.wait_ge(s["lg"], 1)
            ge = [g[:, k, :].rearrange("p (t e) -> p t e", e=E) for k in range(12)]
            ie = iota_e[:, :].rearrange("p (t e) -> p t e", e=E)
            b8 = lambda a: a.rearrange("p (t a) -> p t a", a=1).broadcast_to([P, QT, E])
            lg = bank[:, 2, 0:QT * E].rearrange("p (t e) -> p t e", e=E)
            step(nc.vector.tensor_reduce(g1[:, 0, :], lg, axis=AX.X, op=ALU.max))
            step(nc.vector.tensor_tensor(ge[0], lg, b8(g1[:, 0, :]), ALU.subtract))
            dve.wait_ge(s["gtexp"], 1)
            step(nc.vector.tensor_reduce(g1[:, 1, :], ge[1], axis=AX.X, op=ALU.add))
            step(nc.vector.reciprocal(g1[:, 2, :], g1[:, 1, :]))
            step(nc.vector.tensor_tensor(ge[2], ge[1], b8(g1[:, 2, :]), ALU.mult))
            cur = ge[2]
            for k in range(2):
                step(nc.vector.tensor_reduce(g1[:, 3, :], cur, axis=AX.X, op=ALU.max))
                step(nc.vector.tensor_tensor(ge[3], cur, b8(g1[:, 3, :]), ALU.is_lt))
                step(nc.vector.scalar_tensor_tensor(ge[4], ge[3], 64.0, ie, ALU.mult, ALU.add))
                step(nc.vector.tensor_reduce(g1[:, 4, :], ge[4], axis=AX.X, op=ALU.min))
                step(nc.vector.tensor_tensor(ge[5 + k], ie, b8(g1[:, 4, :]), ALU.is_equal))
                if k == 0:
                    step(nc.vector.scalar_tensor_tensor(ge[7], ge[5], -2.0, ge[2], ALU.mult, ALU.add))
                    cur = ge[7]
            step(nc.vector.tensor_tensor(ge[8], ge[5], ge[6], ALU.add))
            step(nc.vector.tensor_tensor(ge[9], ge[8], ge[2], ALU.mult))
            assert c[0] == GATE_STEPS
            for k in range(2):
                dve.wait_ge(s["gT_ps"], k + 1)
                nc.vector.tensor_copy(epi_e[:, 512 * k:512 * k + 512], bank[0:E, k, :]).then_inc(s["gT_sb"], 1)
            dve.wait_ge(s["b2ps"], 1)
            nc.vector.tensor_tensor(x2, x2, bank[:, 2:4, :].rearrange("p a (t d) -> p (a t) d", d=D), ALU.add).then_inc(s["yacc"], 1)
            for e in range(E):
                for t in range(QT):
                    dve.wait_ge(s["yps"], e * QT + t + 1)
                    dve.wait_ge(s["yacc"], max(1, (e - 1) * QT + t + 2))
                    last = nc.vector.scalar_tensor_tensor(x2[:, t, :], bank[:, 6 + t % 2, 0:P], ge[9][:, t, e:e + 1], x2[:, t, :],
                                                          ALU.mult, ALU.add).then_inc(s["yacc"], 1)

        @block.scalar
        def _(act):
            act.wait_ge(s["ln"], 6)
            nc.scalar.activation(stat[:, 2, :], stat[:, 1, :], ACT.Sqrt).then_inc(s["sqrt"], 1)
            act.wait_ge(s["wt_ps"], 1)
            nc.scalar.activation(wT[:, :, :], bank[:, 4, :].rearrange("p (a b) -> p a b", a=4), ACT.Copy).then_inc(s["wt_sb"], 1)
            act.wait_ge(s["wt_ps"], 2)
            nc.scalar.activation(gateT[:, :], bank[:, 5, 0:E], ACT.Copy).then_inc(s["wt_sb"], 1)
            nc.scalar.activation(b1T[:, :, :], bank[:, 5, 64:64 + FT * E].rearrange("p (a e) -> p a e", a=FT), ACT.Copy).then_inc(s["wt_sb"], 1)
            for k in range(16):
                act.wait_ge(s["wtb_ps"], k + 1)
                dst = w1T[:, k % 8, :, :] if k < 8 else w2T[:, k - 8, :, :]
                nc.scalar.activation(dst, bank[:, 4 + k % 2, :].rearrange("p (a b) -> p a b", a=FT), ACT.Copy).then_inc(s["wtb_sb"], 1)
            act.wait_ge(s["plan_ready"], 1)
            n = act.value_load(plan[0:1, 64:65], min_val=1, max_val=T)
            act.sem_inc(s["ex"], 2)
            with act.Fori(0, n) as i:
                for u in range(16):
                    act.wait_ge(s["qk"], i * 16 + u + 1)
                    act.wait_ge(s["pv"], i * 8 + u // 2 + 1)
                    nc.scalar.activation(arenaB[:, u % 4, :], bank[:, 2 * (u % 2):2 * (u % 2) + 2, :].rearrange("p a b -> p (a b)"),
                                         ACT.Exp, scale=SCALE).then_inc(s["ex"], 1)
            act.wait_ge(s["ln2"], 6)
            nc.scalar.activation(stat[:, 2, :], stat[:, 1, :], ACT.Sqrt).then_inc(s["sqrt2"], 1)
            act.wait_ge(s["gt"], 2)
            nc.scalar.activation(g[:, 1, :], g[:, 0, :], ACT.Exp).then_inc(s["gtexp"], 1)
            for e in range(E):
                for k in range(2 * FT):
                    c = e * 2 * FT + k
                    act.wait_ge(s["hps"], c + 1)
                    if e >= 2 and k == 0:
                        act.wait_ge(s["yps"], (e - 1) * QT)
                    nc.scalar.activation(hT[:, e % 2, k // 2, 512 * (k % 2):512 * (k % 2) + 512], bank[:, 4 + c % 2, :],
                                         ACT.Gelu_apprx_tanh, bias=b1T[:, k // 2, e:e + 1]).then_inc(s["hact"], 1)

        @block.tensor
        def _(pe):
            mm = nc.tensor.matmul
            pe.wait_ge(s["const"], 12)
            pe.wait_ge(s["w_in"], 64)
            for i in range(4):
                last = nc.tensor.transpose(bank[:, 4, i * P:(i + 1) * P], wraw[:, i, :], ident[:, :])
            last.then_inc(s["wt_ps"], 1)
            pe.wait_ge(s["ln"], 12)
            for t in range(QT):
                last = nc.tensor.transpose(bank[:, t // 4, (t % 4) * P:(t % 4 + 1) * P], xn[:, t, :], ident[:, :])
                if t % 4 == 3:
                    last.then_inc(s["xnT_ps"], 1)
            pe.wait_ge(s["wt_sb"], 1)
            pe.wait_ge(s["row_in"], 64)
            for k in range(2):
                pe.wait_ge(s["xT_sb"], k + 1)
                mm(bank[:, 2 + k, :], wT[:, 0, :], xT[:, 512 * k:512 * k + 512], start=True, stop=False)
                last = mm(bank[:, 2 + k, :], brow[0:1, 0, :], ones[0:1, :], start=False, stop=True)
            last.then_inc(s["q_ps"], 1)
            pe.wait_ge(s["gate_in"], 16)
            pe.wait_ge(s["b1_in"], 16)
            last = nc.tensor.transpose(bank[:, 5, 0:E], gate_raw[:, :], ident[0:E, 0:E])
            for a in range(FT):
                last = nc.tensor.transpose(bank[:, 5, 64 + a * E:64 + (a + 1) * E], b1_raw[:, a * P:(a + 1) * P], ident[0:E, 0:E])
            last.then_inc(s["wt_ps"], 1)
            pe.wait_ge(s["wt_sb"], 3)
            pe.wait_ge(s["w1_in"], 16)
            for k in range(16):
                if k >= 2:
                    pe.wait_ge(s["wtb_sb"], k - 1)
                if k == 8:
                    pe.wait_ge(s["w2_in"], 16)
                for a in range(FT):
                    src = w1raw[:, a, k, :] if k < 8 else w2raw[:, k - 8, a * P:(a + 1) * P]
                    last = nc.tensor.transpose(bank[:, 4 + k % 2, a * P:(a + 1) * P], src, ident[:, :])
                last.then_inc(s["wtb_ps"], 1)
            pe.wait_ge(s["pl_sb"], 1)
            mm(b6[0:T, 0:1], cnt4[:, :], ones[:, 0:1], start=True, stop=True).then_inc(s["pl_ps"], 1)
            pe.wait_ge(s["pl_sb"], 2)
            mm(b6[0:T, 1:2], tri[0:T, 0:T], tcol[0:T, 0:1], start=True, stop=True).then_inc(s["pl_ps"], 1)
            pe.wait_ge(s["pl_sb"], 4)
            mm(b6[0:1, 64:128], iota_p[0:T, :], hot[0:T, :], start=True, stop=True)
            mm(b6[0:1, 128:129], tcol[0:T, 0:1], ones[0:T, 0:1], start=True, stop=True).then_inc(s["pl_ps"], 1)
            pe.wait_ge(s["cs_sb"], 1)
            mm(b6[:, 200:201], csum[:, :], ones[:, 0:1], start=True, stop=True).then_inc(s["cs_ps"], 1)
            pe.wait_ge(s["cs_sb"], 2)
            mm(b6[0:1, 256:384], csT[:, :], wT[:, 2, :], start=True, stop=True).then_inc(s["cs_ps"], 1)
            pe.wait_ge(s["cs_sb"], 3)
            mm(b6[:, 384:512], ones[0:1, 0:P], vsrow[0:1, :], start=True, stop=False)
            mm(b6[:, 384:512], s2row[0:1, :], brow[0:1, 2, :], start=False, stop=True).then_inc(s["cs_ps"], 1)
            pe.wait_ge(s["cs_sb"], 4)

            pe.wait_ge(s["plan_ready"], 1)
            pe.wait_ge(s["pl_sb"], 5)
            n = pe.value_load(plan[0:1, 64:65], min_val=1, max_val=T)

            def project(i, cb, ct, ctsb, kv, values):
                pe.wait_ge(cb, i + 1)
                nc.tensor.transpose(b6[:, 0:P], cbuf[:, :], ident[:, :]).then_inc(ct, 1)
                pe.wait_ge(ctsb, i + 1)
                mm(b6[:, P:2 * P], wT[:, 1, :], cT[:, :], start=True, stop=False)
                last = mm(b6[:, P:2 * P], brow[0:1, 1, :], ones[0:1, 0:P], start=False, stop=True)
                if values:
                    mm(b6[:, 2 * P:3 * P], cT[:, :], wT[:, 2, :], start=True, stop=False)
                    last = mm(b6[:, 2 * P:3 * P], ones[0:1, 0:P], brow[0:1, 2, :], start=False, stop=True)
                last.then_inc(kv, 1)

            pe.wait_ge(s["qr"], 16 * NC)
            pe.wait_ge(s["qzero"], 1)
            pe.sem_inc(s["m_ct"], 1)
            pe.sem_inc(s["m_qk"], 1)
            project(0, s["m_cb"], s["m_ct"], s["m_ctsb"], s["m_kv"], False)
            with pe.Fori(0, n) as i:
                pe.wait_ge(s["m_kc"], i + 2)
                pe.wait_ge(s["m_mb"], i + 1)
                for u in range(16):
                    t, hh = u // 2, u % 2
                    pe.wait_ge(s["m_red"], i * 16 + u + 1)
                    for a in range(2):
                        o = bank[:, 2 * hh + a, :]
                        mm(o, nbig[:, :], mbf[:, t, :].rearrange("p (a k) -> p a k", a=1).broadcast_to([P, 4, P]), start=True, stop=False)
                        for b in range(4):
                            h = 8 * hh + 4 * a + b
                            last = mm(o[:, b * P:(b + 1) * P], qS[:, h, t * P:(t + 1) * P], kcur[:, h, :], start=False, stop=(b == 3))
                    last.then_inc(s["m_qk"], 1)
                    if u == 3:
                        pe.wait_ge(s["m_kch"], i * 4 + 4)
                        project(i + 1, s["m_cb"], s["m_ct"], s["m_ctsb"], s["m_kv"], False)
            pe.wait_ge(s["m_fin"], 5)
            pt = bank[:, 0, 0:192].bitcast(BF16)
            for c in range(3):
                last = nc.tensor.transpose(pt[:, c * P:(c + 1) * P], mparts[:, c, :], identb[:, :])
            last.then_inc(s["m_finT"], 1)
            pe.wait_ge(s["m_kch"], n * 4 + 4)

            pe.sem_inc(s["ct"], 1)
            pe.sem_inc(s["pv"], 2)
            pe.sem_inc(s["mt"], 1)

            def scores(i, u, ui, tile_of):
                pe.wait_ge(s["ex"], i * 16 + ui + 1)
                kk = u // 2
                for a in range(2):
                    h = 4 * (kk // 2) + 2 * (u % 2) + a
                    o, cols = bank[:, 2 * (u % 2) + a, :], slice(512 * (kk % 2), 512 * (kk % 2) + 512)
                    mm(o, nbig[:, :], maskT[:, bass.ds(tile_of % 2, 1), cols].rearrange("p a q -> p (a q)"), start=True, stop=False)
                    last = mm(o, kcur[:, h, :], qS[:, h, cols], start=False, stop=True)
                last.then_inc(s["qk"], 1)

            def mask_turn(i):
                pe.wait_ge(s["mb"], i + 1)
                for t in range(QT):
                    last = nc.tensor.transpose(maskT_ps[:, t * P:(t + 1) * P], mbf[:, t, :], identb[:, :])
                last.then_inc(s["mt"], 1)

            project(0, s["cb"], s["ct"], s["ctsb"], s["kv"], True)
            mask_turn(0)
            pe.wait_ge(s["shift"], 48)
            pe.wait_ge(s["kc"], 2)
            pe.wait_ge(s["mc"], 1)
            scores(0, 0, 0, 0)
            scores(0, 1, 1, 0)
            with pe.Fori(0, n) as i:
                for k in range(8):
                    if k == 7:
                        pe.wait_ge(s["kc"], i + 3)
                        pe.wait_ge(s["mc"], i + 2)
                    scores(i, (2 * k + 2) % 16, 2 * k + 2, i + (k == 7))
                    scores(i, (2 * k + 3) % 16, 2 * k + 3, i + (k == 7))
                    pe.wait_ge(s["ex"], i * 16 + 2 * k + 4)
                    pe.wait_ge(s["ac"], i * 8 + k + 1)
                    if k == 0:
                        pe.wait_ge(s["vc"], i + 1)
                    for j in range(4):
                        last = mm(bank[32 * j:32 * j + 32, 4 + k % 2, :], vcur[:, 4 * (k // 2) + j, :],
                                  arenaB[:, (2 * k + j // 2) % 4, 512 * (j % 2):512 * (j % 2) + 512], start=True, stop=True,
                                  tile_position=(0, 32 * j))
                    last.then_inc(s["pv"], 1)
                    if k == 1:
                        pe.wait_ge(s["kch"], i * 4 + 4)
                        project(i + 1, s["cb"], s["ct"], s["ctsb"], s["kv"], True)
                        mask_turn(i + 1)

            pe.wait_ge(s["ac"], n * 8 + 2)
            pe.wait_ge(s["vc"], n + 1)
            for hf in range(2):
                for t in range(4):
                    for gg in range(4):
                        q = (4 * hf + t) * P
                        last = nc.tensor.transpose(bank[:, 4 * hf + t, gg * P:(gg + 1) * P], accU[:, gg, q:q + P], ident[:, :])
                last.then_inc(s["u_ps"], 1)
            for t in range(QT):
                pe.wait_ge(s["u_dve"], 5 * (t // 4) + 5)
                last = nc.tensor.transpose(bank[:, t // 4, (t % 4) * P:(t % 4 + 1) * P], ctxq[:, t, :], ident[:, :])
                if t % 4 == 3:
                    last.then_inc(s["cq_ps"], 1)
            for t in range(QT):
                pe.wait_ge(s["cq_sb"], t // 4 + 1)
                o = bank[:, 2 + t // 4, (t % 4) * P:(t % 4 + 1) * P]
                mm(o, ctxqT[:, t * P:(t + 1) * P], wT[:, 3, :], start=True, stop=False)
                last = mm(o, ones[0:1, 0:P], brow[0:1, 3, :], start=False, stop=True)
            last.then_inc(s["at_ps"], 1)
            pe.wait_ge(s["ln2"], 12)
            for t in range(QT):
                last = nc.tensor.transpose(bank[:, t // 4, (t % 4) * P:(t % 4 + 1) * P], xn2[:, t, :], ident[:, :])
                if t % 4 == 3:
                    last.then_inc(s["x2T_ps"], 1)
            pe.wait_ge(s["x2T_sb"], 2)
            for t in range(QT):
                last = mm(bank[:, 2, t * E:(t + 1) * E], x2T[:, t * P:(t + 1) * P], gateT[:, :], start=True, stop=True)
            last.then_inc(s["lg"], 1)

            def up(e):
                for k in range(2 * FT):
                    c = e * 2 * FT + k
                    if c >= 2:
                        pe.wait_ge(s["hact"], c - 1)
                    mm(bank[:, 4 + c % 2, :], w1T[:, e, k // 2, :], x2T[:, 512 * (k % 2):512 * (k % 2) + 512],
                       start=True, stop=True).then_inc(s["hps"], 1)

            def down(e):
                pe.wait_ge(s["hact"], (e + 1) * 2 * FT)
                for t in range(QT):
                    c = e * QT + t
                    if c >= 2:
                        pe.wait_ge(s["yacc"], c)
                    for a in range(FT):
                        last = mm(bank[:, 6 + t % 2, 0:P], hT[:, e % 2, a, t * P:(t + 1) * P], w2T[:, e, a, :],
                                  start=(a == 0), stop=(a == FT - 1))
                    last.then_inc(s["yps"], 1)

            up(0)
            pe.wait_ge(s["gt"], GATE_STEPS)
            pe.wait_ge(s["b2_in"], 16)
            for t in range(QT):
                last = nc.tensor.transpose(bank[0:E, t // 4, (t % 4) * P:(t % 4 + 1) * P], g[:, 9, t * E:(t + 1) * E], ident[:, :])
                if t % 4 == 3:
                    last.then_inc(s["gT_ps"], 1)
            pe.wait_ge(s["gT_sb"], 2)
            for t in range(QT):
                last = mm(bank[:, 2 + t // 4, (t % 4) * P:(t % 4 + 1) * P], epi_e[:, t * P:(t + 1) * P], b2_sb[:, :], start=True, stop=True)
            last.then_inc(s["b2ps"], 1)
            for e in range(E):
                if e + 1 < E:
                    up(e + 1)
                down(e)


_INS = ['x', 'ctx_1024', 'mask_BxSxS2_bk1', 'L0_xattn_Wq', 'L0_xattn_bq', 'L0_xattn_Wk', 'L0_xattn_bk', 'L0_xattn_Wv',
        'L0_xattn_bv', 'L0_xattn_Wo', 'L0_xattn_bo', 'L0_ffn_gate_w', 'L0_ffn_w1', 'L0_ffn_b1', 'L0_ffn_w2', 'L0_ffn_b2']


def kernel(**inputs):
    import numpy as _np
    import concourse.bacc as _bacc
    from concourse import mybir as _mybir
    from concourse.bass_utils import run_bass_kernel_spmd as _run

    nc = _bacc.Bacc("TRN2", target_bir_lowering=False, num_devices=1)
    arrays, args = {}, []
    for name in _INS:
        a = _np.ascontiguousarray(inputs[name])
        arrays[f"in_{name}_dram"] = a
        args.append(nc.dram_tensor(f"in_{name}_dram", a.shape, _mybir.dt.from_np(a.dtype), kind="ExternalInput").ap())
    args.append(nc.dram_tensor("out_0_dram", (1, S, D), F32, kind="ExternalOutput").ap())
    build(nc, *args)
    r = _run(nc, [arrays], core_ids=[0])
    return r.results[0]["out_0_dram"]
```

```python
import concourse.bass as bass
from concourse import mybir
from contextlib import ExitStack

F32 = mybir.dt.float32
BF16 = mybir.dt.bfloat16
U8 = mybir.dt.uint8
U16 = mybir.dt.uint16
I32 = mybir.dt.int32
ACT = mybir.ActivationFunctionType
ALU = mybir.AluOpType
AX = mybir.AxisListType

P = 128
S, D, H = 1024, 128, 16
HD = D // H
S2 = 6404
E, F = 8, 512
QT = S // P
FT = F // P
T = -(-S2 // P)
PAD = T * P - S2
KW = T * P
SCALE = float(HD) ** -0.5
BIG = 2.0 ** 100
EPS = 1e-5
GATE_STEPS = 18
NC = 9
CHUNKS = -(-T // 4)
BOUND = 40.0
CTX_CUTS = [(1, 12), (12, 24), (24, 36), (36, T)]
SHIFT_ROW = 96


def build(nc, x, ctx_in, mask, Wq, bq, Wk, bk, Wv, bv, Wo, bo, gate_w, w1, b1, w2, b2, out):
    with ExitStack() as es:
        def sb(name, shape, dt):
            return es.enter_context(nc.sbuf_tensor(name, shape, dt))

        def sem(name):
            return es.enter_context(nc.semaphore(name))

        kparts_dram = nc.dram_tensor("kparts_dram", (3, P, P), BF16, kind="Internal").ap()
        qparts_dram = nc.dram_tensor("qparts_dram", (3, P, S), BF16, kind="Internal").ap()

        mask_u8 = sb("mask_u8", [P, QT, KW], U8)
        ctx_sb = sb("ctx_sb", [P, T, D], F32)
        x_sb = sb("x_sb", [P, QT, D], F32)
        arenaA = sb("arenaA", [P, 4096], F32)
        arenaB = sb("arenaB", [P, 4, 1024], F32)
        qS = sb("qS", [P, H, S], BF16)
        arenaC = sb("arenaC", [P, 1664], F32)
        wT = sb("wT", [P, 4, D], F32)
        gateT = sb("gateT", [P, E], F32)
        b1T = sb("b1T", [P, FT, E], F32)
        b2_sb = sb("b2_sb", [E, D], F32)
        w1T = sb("w1T", [P, E, FT, P], F32)
        w2T = sb("w2T", [P, E, FT, D], F32)
        brow = sb("brow", [1, 4, D], F32)
        ones = sb("ones", [P, 512], F32)
        ident = sb("ident", [P, P], F32)
        identb = sb("identb", [P, P], BF16)
        nbig = sb("nbig", [P, P], BF16)
        maskT = sb("maskT", [P, 2, S], BF16)
        stat = sb("stat", [P, 6, QT], F32)
        cbuf = sb("cbuf", [P, D], F32)
        cT = sb("cT", [P, P], F32)
        kres = sb("kres", [P, 2, P], F32)
        kparts = sb("kparts", [P, 3, P], BF16)
        knext = sb("knext", [P, H, P], BF16)
        vcur = sb("vcur", [P, H, 32], F32)
        cnt4 = sb("cnt4", [P, T], F32)
        tcol = sb("tcol", [64, 4], F32)
        headsel = sb("headsel", [P, H], BF16)
        bkcol = sb("bkcol", [P, 1], F32)
        mcount = sb("mcount", [P, 1], F32)
        mixed = sb("mixed", [1, 2], I32)
        norms = sb("norms", [H, 24], F32)
        bound = sb("bound", [1, 4], F32)
        tri = sb("tri", [64, 64], F32)
        iota_s = sb("iota_s", [64, 64], F32)
        iota_p = sb("iota_p", [64, 1], F32)
        hot = sb("hot", [64, 64], F32)
        plan = sb("plan", [1, 72], I32)
        s2row = sb("s2row", [1, P], F32)
        csum = sb("csum", [P, D], F32)
        csT = sb("csT", [P, 1], F32)
        vsrow = sb("vsrow", [1, D], F32)
        vsumB = sb("vsumB", [P, D], F32)
        g1 = sb("g1", [P, 6, QT], F32)
        iota_e = sb("iota_e", [P, QT * E], F32)

        peak = maskT[:, :, :].rearrange("p a q -> p (a q)").bitcast(F32)
        tmax = peak[:, 0:128].rearrange("p (h t) -> p h t", t=QT)
        rmax = peak[:, 768:896].rearrange("p (h t) -> p h t", t=QT)
        mres = peak[:, 128:384].rearrange("p (a k) -> p a k", a=2)
        mparts = peak[:, 384:576].bitcast(BF16).rearrange("p (c k) -> p c k", c=3)
        mpT = peak[:, 576:768].bitcast(BF16).rearrange("p (c k) -> p c k", c=3)

        xn = arenaA[:, 0:1024].rearrange("p (t d) -> p t d", d=D)
        sq = arenaA[:, 1024:2048].rearrange("p (t d) -> p t d", d=D)
        qres = [arenaA[:, 1024:2048]]
        qparts = arenaA[:, 2048:3584].bitcast(BF16).rearrange("p (c q) -> p c q", c=3)
        ctx_cT = w2T[:, :, :, :].rearrange("p e a d -> p (e a d)")[:, 0:1024].rearrange("p (b k) -> p b k", b=2)
        early = w2T[:, :, :, :].rearrange("p e a d -> p (e a d)")
        xT = early[:, 0:1024]
        wraw = early[:, 1024:1536].rearrange("p (a d) -> p a d", a=4)
        gate_raw = early[0:E, 1536:1664]
        b1_raw = early[0:E, 1664:2176]
        and_acc = arenaC[:, 0:KW // 4].bitcast(I32)
        kcur = arenaC[:, 0:1024].bitcast(BF16).rearrange("p (h k) -> p h k", h=H)
        mbf = arenaC[:, 1024:1536].bitcast(BF16).rearrange("p (t k) -> p t k", t=QT)
        w2raw = qS[:, 0:8, :].rearrange("p h q -> p (h q)").bitcast(F32).rearrange("p (e f) -> p e f", e=E)
        accU = arenaA[:, :].rearrange("p (g q) -> p g q", g=4)
        w1raw = arenaB[:, :, :].rearrange("p a (e d) -> p a e d", e=E)
        after = ctx_sb[:, :, :].rearrange("p t d -> p (t d)")
        x2 = after[:, 0:1024].rearrange("p (t d) -> p t d", d=D)
        xn2 = after[:, 1024:2048].rearrange("p (t d) -> p t d", d=D)
        x2T = after[:, 2048:3072]
        ctxq = after[:, 3072:4096].rearrange("p (t d) -> p t d", d=D)
        ctxqT = after[:, 4096:5120]
        sq2 = after[:, 5120:6144].rearrange("p (t d) -> p t d", d=D)
        g = after[:, 5120:5888].rearrange("p (a b) -> p a b", a=12)
        epi_e = after[0:E, 3072:4096]
        squares = early[:, 2176:2688].bitcast(BF16).rearrange("p (b k) -> p b k", b=2)
        hT = mask_u8[:, :, :].rearrange("p t k -> p (t k)").bitcast(F32)[:, 0:8192].rearrange(
            "p (b t q) -> p b t q", b=2, t=FT)
        maskw = mask_u8[:, :, :].bitcast(I32)

        bank = es.enter_context(nc.psum_tensor("bank", [P, 8, 512], F32))
        maskT_ps = bank[:, 7, :].bitcast(BF16)
        b6 = bank[:, 6, :]

        names = ("x_in w_in row_in gate_in b1_in b2_in w1_in w2_in ctx_in ctxpad mask_in pad const ln "
                 "sqrt xnT_ps xT_sb q_ps q_sb qw qr qzero wt_ps wt_sb wtb_ps wtb_sb "
                 "and_ cs cs_ps cs_sb pl_ps pl_sb plan_ready act_ev pe_w acc0 "
                 "m_cb m_ct m_ctsb m_kv m_kch m_kw m_kr m_kc m_mb m_qk m_red m_max m_fin m_finT m_finsb shift "
                 "cb ct ctsb kv kch kw kr kc vc mb mt mc cm fl qk ex pv ac "
                 "u_ps u_dve cq_ps cq_sb at_ps x2s ln2 sqrt2 x2T_ps x2T_sb lg gt gtexp gT_ps gT_sb "
                 "hps hact yps yacc b2ps moe outs kinit vinit fin_x sp_at pool_at dve_at pe_at hs qn_ps qn kn_ps kn bd bd_ps bd_sqrt bd_row kones sqr cc_ps cc_sb kk_ps").split()
        s = {n: sem(n) for n in names}
        ctx_in_s = [sem(f"ctx_in{k}") for k in range(len(CTX_CUTS))]
        mask_in = [sem(f"mask_in{t}") for t in range(QT)]

        block = es.enter_context(nc.Block())

        @block.sync
        def _(sp):
            sp.dma_start(x_sb[:, :, :], x.rearrange("a (p t) d -> p (a t) d", t=QT)).then_inc(s["x_in"], 16)
            for i, w in enumerate((Wq, Wk, Wv, Wo)):
                sp.dma_start(wraw[:, i, :], w).then_inc(s["w_in"], 16)
            sp.dma_start(bkcol[:, :], bk.rearrange("(n a) -> n a", a=1)).then_inc(s["row_in"], 16)
            for i, b in enumerate((bq, bk, bv, bo)):
                sp.dma_start(brow[0:1, i, :], b.rearrange("(a n) -> a n", a=1)).then_inc(s["row_in"], 16)
            c = ctx_in[0, P - PAD:S2, :].rearrange("(t p) d -> p t d", p=P)
            for k, (t0, t1) in enumerate(CTX_CUTS):
                sp.dma_start(ctx_sb[:, t0:t1, :], c[:, t0 - 1:t1 - 1, :]).then_inc(ctx_in_s[k], 16)
            sp.wait_ge(s["q_sb"], 4)
            sp.dma_start(qparts_dram.rearrange("c p q -> p c q"), qparts[:, :, :]).then_inc(s["qw"], 16)
            sp.wait_ge(s["qw"], 16)
            sp.wait_ge(s["qzero"], 1)
            for c in range(NC):
                sp.dma_start(qS[c * HD:(c + 1) * HD, :, :],
                             qparts_dram[c // 3, :, :].rearrange("(h d) q -> d h q", d=HD)).then_inc(s["qr"], 16)

            def key_rows(i, chain, written, read, copied):
                sp.wait_ge(chain, i * 4 + 4)
                sp.dma_start(kparts_dram.rearrange("c p k -> p c k"), kparts[:, :, :]).then_inc(written, 16)
                sp.wait_ge(written, i * 16 + 16)
                sp.sem_inc(s["sp_at"], 1)
                sp.wait_ge(copied, i + 1)
                for c in range(NC):
                    sp.dma_start(knext[c * HD:(c + 1) * HD, :, :],
                                 kparts_dram[c % 3, :, :].rearrange("(h d) k -> d h k", d=HD)).then_inc(read, 16)

            sp.wait_ge(s["plan_ready"], 1)
            n = sp.value_load(plan[0:1, 64:65], min_val=1, max_val=T)
            sp.wait_ge(s["kinit"], 1)
            general = sp.value_load(plan[0:1, 65:66], min_val=0, max_val=1)
            with sp.If(general):
                with sp.Fori(0, n + 1) as i:
                    key_rows(i, s["m_kch"], s["m_kw"], s["m_kr"], s["m_kc"])
                sp.wait_ge(s["m_kr"], n * 144 + 144)
                sp.sem_inc(s["sp_at"], 1)
                for c in range(3):
                    sp.wait_ge(s["m_finsb"], 1)
                    sp.dma_start(qS[SHIFT_ROW + 1 + c:SHIFT_ROW + 2 + c, :, :].rearrange("a h (t q) -> a (h t) q", q=P),
                                 mpT[:, c, :]).then_inc(s["shift"], 16)
            with sp.Fori(0, n + 1) as i:
                key_rows(i, s["kch"], s["kw"], s["kr"], s["kc"])
            sp.wait_ge(s["ac"], n * 8 + 2)
            sp.sem_inc(s["sp_at"], 1)
            sp.wait_ge(s["vc"], n + 1)
            sp.sem_inc(s["sp_at"], 1)
            sp.wait_ge(s["qk"], n * 16 + 2)
            sp.dma_start(w1raw, w1.rearrange("(a p) e d -> p a e d", p=P)).then_inc(s["w1_in"], 16)
            sp.dma_start(w2raw, w2).then_inc(s["w2_in"], 16)
            sp.wait_ge(s["yacc"], E * QT + 1)
            sp.dma_start(out.rearrange("a (p t) d -> p (a t) d", t=QT), x2).then_inc(s["outs"], 16)
            sp.wait_ge(s["outs"], 16)

        @block.gpsimd
        def _(pool):
            pool.dma_start(gate_raw[:, :], gate_w).then_inc(s["gate_in"], 16)
            pool.dma_start(b1_raw[:, :], b1).then_inc(s["b1_in"], 16)
            pool.dma_start(b2_sb[:, :], b2).then_inc(s["b2_in"], 16)
            nc.gpsimd.memset(ident[:, :], 0.0).then_inc(s["const"], 1)
            pool.wait_ge(s["const"], 1)
            nc.gpsimd.affine_select(out=ident[:, :], in_=ident[:, :], compare_op=ALU.not_equal, fill=1.0,
                                    base=0, pattern=[[-1, P]], channel_multiplier=1).then_inc(s["const"], 1)
            nc.gpsimd.memset(ones[:, :], 1.0).then_inc(s["const"], 1)
            nc.gpsimd.memset(s2row[:, :], float(S2)).then_inc(s["const"], 1)
            pool.wait_ge(s["const"], 4)
            nc.gpsimd.tensor_copy(identb[:, :], ident[:, :]).then_inc(s["const"], 1)
            nc.gpsimd.memset(nbig[:, :], 0.0).then_inc(s["const"], 1)
            nc.gpsimd.memset(tri[:, :], 1.0).then_inc(s["const"], 1)
            pool.wait_ge(s["const"], 7)
            nc.gpsimd.affine_select(out=nbig[:, :], in_=nbig[:, :], compare_op=ALU.not_equal, fill=-BIG,
                                    base=0, pattern=[[-1, P]], channel_multiplier=1).then_inc(s["const"], 1)
            nc.gpsimd.affine_select(out=tri[:, :], in_=tri[:, :], compare_op=ALU.is_gt, fill=0.0,
                                    base=0, pattern=[[1, 64]], channel_multiplier=-1).then_inc(s["const"], 1)
            nc.gpsimd.iota(iota_s[:, :], [[1, 64]], base=0, channel_multiplier=0,
                           allow_small_or_imprecise_dtypes=True).then_inc(s["const"], 1)
            nc.gpsimd.iota(iota_p[:, :], [[0, 1]], base=0, channel_multiplier=1,
                           allow_small_or_imprecise_dtypes=True).then_inc(s["const"], 1)
            nc.gpsimd.iota(iota_e[:, :], [[0, QT], [1, E]], base=0, channel_multiplier=0,
                           allow_small_or_imprecise_dtypes=True).then_inc(s["const"], 1)
            nc.gpsimd.memset(mask_u8[:, :, 0:PAD], 1).then_inc(s["pad"], 1)
            nc.gpsimd.memset(ctx_sb[:, 0, :], 0.0).then_inc(s["ctxpad"], 1)
            pool.wait_ge(s["ctxpad"], 1)
            pool.dma_start(ctx_sb[PAD:P, 0, :], ctx_in[0, 0:P - PAD, :]).then_inc(s["ctx_in"], 16)
            nc.gpsimd.memset(qS[64:P, :, :].bitcast(F32), 0.0).then_inc(s["qzero"], 1)
            pool.wait_ge(s["qzero"], 1)
            nc.gpsimd.memset(knext[64:P, :, :].bitcast(F32), 0.0).then_inc(s["qzero"], 1)
            pool.wait_ge(s["qzero"], 2)
            nc.gpsimd.memset(knext[SHIFT_ROW:SHIFT_ROW + 4, :, :], 1.0).then_inc(s["kones"], 1)
            pool.wait_ge(s["kones"], 1)
            nc.gpsimd.memset(qS[SHIFT_ROW:SHIFT_ROW + 1, :, :], 1.0).then_inc(s["qzero"], 1)
            pool.wait_ge(s["qzero"], 3)
            nc.gpsimd.memset(vcur[:, :, :], 0.0).then_inc(s["qzero"], 1)
            pool.wait_ge(s["qzero"], 4)
            nc.gpsimd.memset(vcur[:, :, HD:HD + 1], 1.0).then_inc(s["vinit"], 1)

            pool.wait_ge(s["qw"], 16)
            nc.gpsimd.memset(arenaA[:, :], 0.0).then_inc(s["ac"], 1)
            pool.wait_ge(s["plan_ready"], 1)
            n = pool.value_load(plan[0:1, 64:65], min_val=1, max_val=T)

            def tile_in(i, cb, ct, mb, mask_used, per_tile):
                tile = pool.value_load(plan[0:1, bass.ds(i, 1)], min_val=0, max_val=T - 1)
                pool.wait_ge(ct, i + 1)
                nc.gpsimd.tensor_copy(cbuf[:, :], ctx_sb[:, bass.ds(tile, 1), :].rearrange("p a d -> p (a d)")).then_inc(cb, 1)
                pool.wait_ge(mask_used, i * per_tile + 1)
                nc.gpsimd.tensor_copy(mbf[:, :, :], mask_u8[:, :, bass.ds(tile * P, P)]).then_inc(mb, 1)

            general = pool.value_load(plan[0:1, 65:66], min_val=0, max_val=1)
            with pool.If(general):
                with pool.Fori(0, n + 1) as i:
                    tile_in(i, s["m_cb"], s["m_ct"], s["m_mb"], s["m_qk"], 16)
                pool.wait_ge(s["m_ct"], n + 2)
                pool.sem_inc(s["pool_at"], 1)
                pool.wait_ge(s["m_mb"], n + 1)
                pool.sem_inc(s["pool_at"], 1)
            with pool.Fori(0, n + 1) as i:
                tile_in(i, s["cb"], s["ct"], s["mb"], s["mt"], 1)

        def layer_norm(dve, xin, xout, scratch, done, sqrt_done):
            c = [0]

            def step(ins):
                c[0] += 1
                ins.then_inc(done, 1)
                dve.wait_ge(done, c[0])

            mean, var, root, inv, t1 = (stat[:, k, :] for k in range(5))
            step(nc.vector.tensor_reduce(mean, xin, axis=AX.X, op=ALU.add))
            step(nc.vector.tensor_scalar(mean, mean, 1.0 / D, None, ALU.mult))
            step(nc.vector.tensor_tensor(xout, xin, mean.rearrange("p (t a) -> p t a", a=1).broadcast_to([P, QT, D]), ALU.subtract))
            step(nc.vector.tensor_tensor(scratch, xout, xout, ALU.mult))
            step(nc.vector.tensor_reduce(var, scratch, axis=AX.X, op=ALU.add))
            step(nc.vector.tensor_scalar(var, var, 1.0 / D, EPS, ALU.mult, ALU.add))
            dve.wait_ge(sqrt_done, 1)
            step(nc.vector.reciprocal(inv, root))
            step(nc.vector.tensor_tensor(t1, var, inv, ALU.mult))
            step(nc.vector.tensor_tensor(t1, t1, root, ALU.add))
            step(nc.vector.tensor_scalar(t1, t1, 0.5, None, ALU.mult))
            step(nc.vector.reciprocal(inv, t1))
            nc.vector.tensor_tensor(xout, xout, inv.rearrange("p (t a) -> p t a", a=1).broadcast_to([P, QT, D]), ALU.mult).then_inc(done, 1)

        def parts3(dve, dst, src, res, chain, base):
            nc.vector.tensor_copy(dst[0], src).then_inc(chain, 1)
            dve.wait_ge(chain, base + 1)
            nc.vector.tensor_tensor(res[0], src, dst[0], ALU.subtract).then_inc(chain, 1)
            dve.wait_ge(chain, base + 2)
            nc.vector.tensor_copy(dst[1], res[0]).then_inc(chain, 1)
            dve.wait_ge(chain, base + 3)
            nc.vector.tensor_tensor(dst[2], res[0], dst[1], ALU.subtract).then_inc(chain, 1)

        @block.vector
        def _(dve):
            dve.wait_ge(s["x_in"], 16)
            layer_norm(dve, x_sb[:, :, :], xn, sq, s["ln"], s["sqrt"])
            for k in range(2):
                dve.wait_ge(s["xnT_ps"], k + 1)
                nc.vector.tensor_copy(xT[:, 512 * k:512 * k + 512], bank[:, k, :]).then_inc(s["xT_sb"], 1)
            dve.wait_ge(s["q_ps"], 1)
            qp = bank[:, 2:4, :].rearrange("p a b -> p (a b)")
            parts3(dve, [qparts[:, k, :] for k in range(3)], qp, [qres[0]], s["q_sb"], 0)

            dve.wait_ge(s["ctx_in"], 16)
            for k in range(len(CTX_CUTS)):
                dve.wait_ge(ctx_in_s[k], 16)
            nc.vector.tensor_reduce(csum[:, :], ctx_sb[:, :, :].rearrange("p t d -> p d t"), axis=AX.X, op=ALU.add).then_inc(s["cs_sb"], 1)
            dve.wait_ge(s["const"], 12)
            nc.vector.tensor_reduce(headsel[:, :], identb[:, :].rearrange("p (h d) -> p h d", d=HD), axis=AX.X, op=ALU.max).then_inc(s["hs"], 1)
            dve.wait_ge(s["qn_ps"], 1)
            nc.vector.tensor_reduce(norms[:, 16:18], bank[0:H, 6:8, :], axis=AX.X, op=ALU.max).then_inc(s["qn"], 1)

            def key_norms(c):
                dve.wait_ge(s["kn_ps"], c + 1)
                nc.vector.tensor_reduce(norms[:, c:c + 1], bank[0:H, 2 + c % 2, 0:min(512, KW - 512 * c)], axis=AX.X, op=ALU.max).then_inc(s["kn"], 1)

            dve.wait_ge(s["pad"], 1)
            dve.wait_ge(mask_in[0], 16)
            for t in range(1, QT):
                dve.wait_ge(mask_in[t], 16)
                if t > 1:
                    dve.wait_ge(s["and_"], t - 1)
                for k in range(2 * t - 2, 2 * t if t < QT - 1 else CHUNKS):
                    key_norms(k)
                nc.vector.tensor_tensor(and_acc[:, :], maskw[:, 0, :] if t == 1 else and_acc[:, :], maskw[:, t, :],
                                        ALU.bitwise_and).then_inc(s["and_"], 1)
            c = QT - 1
            w = P // 4
            dve.wait_ge(s["kn"], CHUNKS)
            nc.vector.tensor_reduce(norms[:, 18:19], norms[:, 0:CHUNKS], axis=AX.X, op=ALU.max).then_inc(s["bd"], 1)
            nc.vector.tensor_reduce(norms[:, 19:20], norms[:, 16:18], axis=AX.X, op=ALU.max).then_inc(s["bd"], 1)
            dve.wait_ge(s["bd"], 2)
            nc.vector.tensor_tensor(norms[:, 20:21], norms[:, 18:19], norms[:, 19:20], ALU.mult).then_inc(s["bd"], 1)
            av = and_acc[:, :].rearrange("p (t w) -> p t w", w=w)
            while w > 1:
                w //= 2
                dve.wait_ge(s["and_"], c)
                nc.vector.tensor_tensor(av[:, :, 0:w], av[:, :, 0:w], av[:, :, w:2 * w], ALU.bitwise_and).then_inc(s["and_"], 1)
                c += 1
            dve.wait_ge(s["and_"], c)
            ab = and_acc[:, :].bitcast(U8).rearrange("p (t b) -> p t b", b=P)[:, :, 0:4]
            nc.vector.tensor_reduce(cnt4[:, :], ab, axis=AX.X, op=ALU.add).then_inc(s["pl_sb"], 1)
            dve.wait_ge(s["pl_ps"], 1)
            nc.vector.tensor_scalar(tcol[0:T, 0:1], b6[0:T, 0:1], 4.0 * P - 0.5, None, ALU.is_lt).then_inc(s["pl_sb"], 1)
            dve.wait_ge(s["pl_ps"], 2)
            nc.vector.tensor_copy(tcol[0:T, 1:2], b6[0:T, 1:2]).then_inc(s["pl_sb"], 1)
            dve.wait_ge(s["pl_sb"], 3)
            nc.vector.tensor_scalar(hot[0:T, :], iota_s[0:T, :], tcol[0:T, 1:2], tcol[0:T, 0:1], ALU.is_equal, ALU.mult).then_inc(s["pl_sb"], 1)
            dve.wait_ge(s["pl_ps"], 3)
            nc.vector.tensor_copy(plan[0:1, 0:64], b6[0:1, 64:128]).then_inc(s["pl_sb"], 1)
            nc.vector.tensor_scalar(plan[0:1, 64:65], b6[0:1, 128:129], 1.0, None, ALU.max).then_inc(s["pl_sb"], 1)

            dve.wait_ge(s["bd_ps"], 1)
            nc.vector.tensor_reduce(bound[:, 0:1], bank[0:1, 4, 0:H], axis=AX.X, op=ALU.max).then_inc(s["bd"], 1)
            dve.wait_ge(s["bd_sqrt"], 1)
            nc.vector.tensor_scalar(bound[:, 2:3], bound[:, 1:2], BOUND / SCALE, None, ALU.is_le).then_inc(s["bd"], 1)
            dve.wait_ge(s["bd"], 5)
            nc.vector.tensor_scalar(plan[0:1, 65:66], bound[:, 2:3], -1.0, 1.0, ALU.mult, ALU.add).then_inc(s["bd"], 1)
            nc.vector.scalar_tensor_tensor(bound[:, 3:4], bound[:, 1:2], -1.0, bound[:, 2:3], ALU.mult, ALU.mult).then_inc(s["plan_ready"], 1)

            dve.wait_ge(s["plan_ready"], 1)
            dve.wait_ge(s["bd_row"], 1)
            dve.wait_ge(s["kones"], 1)
            nc.vector.tensor_copy(knext[SHIFT_ROW:SHIFT_ROW + 1, :, :].rearrange("p h k -> p (h k)"), bank[SHIFT_ROW:SHIFT_ROW + 1, 7, 0:1].broadcast_to([1, H * P])).then_inc(s["kinit"], 1)
            n = dve.value_load(plan[0:1, 64:65], min_val=1, max_val=T)
            def key_parts(i, ct, ctsb, kv, kch):
                dve.wait_ge(ct, i + 2)
                nc.vector.tensor_copy(cT[:, :], b6[:, 0:P]).then_inc(ctsb, 1)
                dve.wait_ge(kv, i + 1)
                parts3(dve, [kparts[:, k, :] for k in range(3)], b6[:, P:2 * P], [kres[:, 0, :]], kch, i * 4)

            general = dve.value_load(plan[0:1, 65:66], min_val=0, max_val=1)
            with dve.If(general):
                nc.vector.memset(rmax[:, :, :], -4.0 * BIG).then_inc(s["m_max"], 1)

                dve.sem_inc(s["m_kc"], 1)
                dve.sem_inc(s["m_red"], 2)

                def key_parts_max(i):
                    key_parts(i, s["m_ct"], s["m_ctsb"], s["m_kv"], s["m_kch"])

                key_parts_max(0)
                with dve.Fori(0, n) as i:
                    dve.wait_ge(s["m_kr"], i * 144 + 144)
                    dve.wait_ge(s["m_qk"], i * 16 + 1)
                    nc.vector.tensor_copy(kcur[:, :, :], knext[:, :, :]).then_inc(s["m_kc"], 1)
                    for u in range(16):
                        t, hh = u // 2, u % 2
                        dve.wait_ge(s["m_qk"], i * 16 + u + 2)
                        if u == 0:
                            dve.wait_ge(s["m_max"], i + 1)
                        nc.vector.tensor_reduce(tmax[:, 8 * hh:8 * hh + 8, t], bank[:, 2 * hh:2 * hh + 2, :].rearrange("p a (h k) -> p (a h) k", k=P),
                                                axis=AX.X, op=ALU.max).then_inc(s["m_red"], 1)
                        if u == 3:
                            dve.wait_ge(s["m_kw"], i * 16 + 16)
                            key_parts_max(i + 1)
                    dve.wait_ge(s["m_red"], i * 16 + 18)
                    nc.vector.tensor_tensor(rmax[:, :, :], rmax[:, :, :], tmax[:, :, :], ALU.max).then_inc(s["m_max"], 1)
                dve.wait_ge(s["m_max"], n + 1)
                m2 = rmax[:, :, :].rearrange("p h t -> p (h t)")
                nc.vector.tensor_scalar(mres[:, 0, :], m2, -BIG / 4, -1.0, ALU.max, ALU.mult).then_inc(s["m_fin"], 1)
                dve.wait_ge(s["m_fin"], 1)
                parts3(dve, [mparts[:, k, :] for k in range(3)], mres[:, 0, :], [mres[:, 1, :]], s["m_fin"], 1)
                dve.wait_ge(s["m_finT"], 1)
                nc.vector.tensor_copy(mpT[:, :, :], bank[:, 0, 0:192].bitcast(BF16).rearrange("p (c q) -> p c q", c=3)).then_inc(s["m_finsb"], 1)
                dve.wait_ge(s["m_kr"], n * 144 + 144)
                dve.wait_ge(s["shift"], 48)

                dve.wait_ge(s["m_kw"], n * 16 + 16)
                dve.sem_inc(s["dve_at"], 1)
            dve.sem_inc(s["kc"], 1)

            def parts(i):
                key_parts(i, s["ct"], s["ctsb"], s["kv"], s["kch"])

            def key_copy(i):
                dve.wait_ge(s["kr"], i * 144 + 144)
                nc.vector.tensor_copy(kcur[:, :, :], knext[:, :, :]).then_inc(s["kc"], 1)

            def mask_copy(i):
                dve.wait_ge(s["mt"], i + 2)
                nc.vector.tensor_scalar(maskT[:, bass.ds(i % 2, 1), :], maskT_ps.rearrange("p (a q) -> p a q", a=1), 1.0, None,
                                        ALU.mult, ALU.add, accum_out=mcount[:, :]).then_inc(s["mc"], 1)

            def mask_flag(i):
                dve.wait_ge(s["cm"], i + 1)
                nc.vector.tensor_scalar(mixed[0:1, bass.ds(i % 2, 1)], bank[0:1, 7, 0:1], 1.0, None, ALU.min).then_inc(s["fl"], 1)

            def value_copy():
                nc.vector.tensor_copy(vcur[:, :, 0:HD], b6[:, 2 * P:3 * P].rearrange("p (h d) -> p h d", d=HD)).then_inc(s["vc"], 1)

            def add(i, k):
                dve.wait_ge(s["pv"], i * 8 + k + 3)
                dve.wait_ge(s["ac"], i * 8 + k + 2)
                a = accU[:, k // 2, 512 * (k % 2):512 * (k % 2) + 512]
                nc.vector.tensor_tensor(a, bank[:, 4 + k % 2, :], a, ALU.add).then_inc(s["ac"], 1)

            dve.sem_inc(s["ac"], 1)
            parts(0)
            key_copy(0)
            dve.wait_ge(s["vinit"], 1)
            value_copy()
            mask_copy(0)
            mask_flag(0)
            with dve.Fori(0, n) as i:
                for k in range(8):
                    if k >= 1:
                        add(i, k - 1)
                    if k == 2:
                        dve.wait_ge(s["kw"], i * 16 + 16)
                        parts(i + 1)
                        mask_copy(i + 1)
                    if k == 4:
                        mask_flag(i + 1)
                    if k == 6:
                        dve.wait_ge(s["qk"], i * 16 + 16)
                        key_copy(i + 1)
                add(i, 7)
                value_copy()
            dve.wait_ge(s["ac"], n * 8 + 2)
            nc.vector.memset(stat[:, 5, :], 0.0).then_inc(s["fin_x"], 1)

            dve.wait_ge(s["cs_ps"], 1)
            nc.vector.tensor_copy(csT[:, :], b6[:, 200:201]).then_inc(s["cs_sb"], 1)
            dve.wait_ge(s["cs_ps"], 2)
            nc.vector.tensor_copy(vsrow[:, :], b6[0:1, 256:384]).then_inc(s["cs_sb"], 1)
            dve.wait_ge(s["cs_ps"], 3)
            nc.vector.tensor_copy(vsumB[:, :], b6[:, 384:512]).then_inc(s["cs_sb"], 1)

            for hf in range(2):
                dve.wait_ge(s["u_ps"], hf + 1)
                U = bank[:, 4 * hf:4 * hf + 4, :].rearrange("p t (k c) -> p (t k) c", c=32)
                c0 = 5 * hf
                flag, weight, inv, tmp = (after[:, 5120 + 64 * k:5120 + 64 * k + (512 if k == 3 else 64)] for k in range(4))
                cq = ctxq[:, 4 * hf:4 * hf + 4, :].rearrange("p t (h c) -> p (t h) c", c=HD)
                tmp = tmp.rearrange("p (k c) -> p k c", c=HD)
                over = lambda a: a.rearrange("p (k a) -> p k a", a=1).broadcast_to([P, 64, HD])
                if hf:
                    dve.wait_ge(s["u_dve"], 5)
                nc.vector.tensor_scalar(flag, U[:, :, HD], 0.0, None, ALU.is_equal).then_inc(s["u_dve"], 1)
                dve.wait_ge(s["u_dve"], c0 + 1)
                nc.vector.scalar_tensor_tensor(weight, flag, float(S2), U[:, :, HD], ALU.mult, ALU.add).then_inc(s["u_dve"], 1)
                for t in range(4):
                    last = nc.vector.tensor_tensor(tmp[:, H * t:H * t + H, :], over(flag)[:, H * t:H * t + H, :],
                                                   vsumB[:, :].rearrange("p (h c) -> p h c", c=HD), ALU.mult)
                last.then_inc(s["u_dve"], 1)
                dve.wait_ge(s["u_dve"], c0 + 3)
                nc.vector.tensor_tensor(cq, tmp, U[:, :, 0:HD], ALU.add)
                nc.vector.reciprocal(inv, weight).then_inc(s["u_dve"], 1)
                dve.wait_ge(s["u_dve"], c0 + 4)
                nc.vector.tensor_tensor(cq, cq, over(inv), ALU.mult).then_inc(s["u_dve"], 1)
            for k in range(2):
                dve.wait_ge(s["cq_ps"], k + 1)
                nc.vector.tensor_copy(ctxqT[:, 512 * k:512 * k + 512], bank[:, k, :]).then_inc(s["cq_sb"], 1)
            dve.wait_ge(s["at_ps"], 1)
            nc.vector.tensor_tensor(x2, x_sb[:, :, :], bank[:, 2:4, :].rearrange("p a (t d) -> p (a t) d", d=D), ALU.add).then_inc(s["x2s"], 1)
            dve.wait_ge(s["x2s"], 1)
            layer_norm(dve, x2, xn2, sq2, s["ln2"], s["sqrt2"])
            for k in range(2):
                dve.wait_ge(s["x2T_ps"], k + 1)
                nc.vector.tensor_copy(x2T[:, 512 * k:512 * k + 512], bank[:, k, :]).then_inc(s["x2T_sb"], 1)

            c = [0]

            def step(ins):
                c[0] += 1
                ins.then_inc(s["gt"], 1)
                dve.wait_ge(s["gt"], c[0])

            dve.wait_ge(s["lg"], 1)
            ge = [g[:, k, :].rearrange("p (t e) -> p t e", e=E) for k in range(12)]
            ie = iota_e[:, :].rearrange("p (t e) -> p t e", e=E)
            b8 = lambda a: a.rearrange("p (t a) -> p t a", a=1).broadcast_to([P, QT, E])
            lg = bank[:, 2, 0:QT * E].rearrange("p (t e) -> p t e", e=E)
            step(nc.vector.tensor_reduce(g1[:, 0, :], lg, axis=AX.X, op=ALU.max))
            step(nc.vector.tensor_tensor(ge[0], lg, b8(g1[:, 0, :]), ALU.subtract))
            dve.wait_ge(s["gtexp"], 1)
            step(nc.vector.tensor_reduce(g1[:, 1, :], ge[1], axis=AX.X, op=ALU.add))
            step(nc.vector.reciprocal(g1[:, 2, :], g1[:, 1, :]))
            step(nc.vector.tensor_tensor(ge[2], ge[1], b8(g1[:, 2, :]), ALU.mult))
            cur = ge[2]
            for k in range(2):
                step(nc.vector.tensor_reduce(g1[:, 3, :], cur, axis=AX.X, op=ALU.max))
                step(nc.vector.tensor_tensor(ge[3], cur, b8(g1[:, 3, :]), ALU.is_lt))
                step(nc.vector.scalar_tensor_tensor(ge[4], ge[3], 64.0, ie, ALU.mult, ALU.add))
                step(nc.vector.tensor_reduce(g1[:, 4, :], ge[4], axis=AX.X, op=ALU.min))
                step(nc.vector.tensor_tensor(ge[5 + k], ie, b8(g1[:, 4, :]), ALU.is_equal))
                if k == 0:
                    step(nc.vector.scalar_tensor_tensor(ge[7], ge[5], -2.0, ge[2], ALU.mult, ALU.add))
                    cur = ge[7]
            step(nc.vector.tensor_tensor(ge[8], ge[5], ge[6], ALU.add))
            step(nc.vector.tensor_tensor(ge[9], ge[8], ge[2], ALU.mult))
            assert c[0] == GATE_STEPS
            for k in range(2):
                dve.wait_ge(s["gT_ps"], k + 1)
                nc.vector.tensor_copy(epi_e[:, 512 * k:512 * k + 512], bank[0:E, k, :]).then_inc(s["gT_sb"], 1)
            dve.wait_ge(s["b2ps"], 1)
            nc.vector.tensor_tensor(x2, x2, bank[:, 2:4, :].rearrange("p a (t d) -> p (a t) d", d=D), ALU.add).then_inc(s["yacc"], 1)
            for e in range(E):
                for t in range(QT):
                    dve.wait_ge(s["yps"], e * QT + t + 1)
                    dve.wait_ge(s["yacc"], max(1, (e - 1) * QT + t + 2))
                    last = nc.vector.scalar_tensor_tensor(x2[:, t, :], bank[:, 6 + t % 2, 0:P], ge[9][:, t, e:e + 1], x2[:, t, :],
                                                          ALU.mult, ALU.add).then_inc(s["yacc"], 1)

        @block.scalar
        def _(act):
            m = mask.rearrange("a (p t) k -> p (a t) k", t=QT)
            for t in range(QT):
                act.dma_start(mask_u8[:, t, PAD:KW], m[:, t, :]).then_inc(mask_in[t], 16)
            act.wait_ge(s["ln"], 6)
            nc.scalar.activation(stat[:, 2, :], stat[:, 1, :], ACT.Sqrt).then_inc(s["sqrt"], 1)
            act.wait_ge(s["wt_ps"], 1)
            nc.scalar.activation(wT[:, :, :], bank[:, 4, :].rearrange("p (a b) -> p a b", a=4), ACT.Copy).then_inc(s["wt_sb"], 1)
            act.wait_ge(s["wt_ps"], 2)
            nc.scalar.activation(gateT[:, :], bank[:, 5, 0:E], ACT.Copy).then_inc(s["wt_sb"], 1)
            nc.scalar.activation(b1T[:, :, :], bank[:, 5, 64:64 + FT * E].rearrange("p (a e) -> p a e", a=FT), ACT.Copy).then_inc(s["wt_sb"], 1)
            act.wait_ge(s["q_sb"], 2)
            act.wait_ge(s["row_in"], 80)
            for k in range(2):
                nc.scalar.activation(squares[:, k, :], bank[:, 2 + k, :], ACT.Square).then_inc(s["sqr"], 1)
            for c in range(CHUNKS + 1):
                if c < CHUNKS:
                    w = min(512, KW - 512 * c)
                    act.wait_ge(s["cc_ps"], c + 1)
                    nc.scalar.activation(ctx_cT[:, c % 2, 0:w], bank[:, c % 2, 0:w], ACT.Copy).then_inc(s["cc_sb"], 1)
                if c >= 1:
                    w = min(512, KW - 512 * (c - 1))
                    act.wait_ge(s["kk_ps"], c)
                    if c < 3:
                        act.wait_ge(s["qn_ps"], 1)
                    else:
                        act.wait_ge(s["kn_ps"], c - 2)
                    nc.scalar.activation(squares[:, (c - 1) % 2, 0:w], bank[:, 6 + (c - 1) % 2, 0:w], ACT.Square, bias=bkcol[:, :]).then_inc(s["sqr"], 1)
            act.wait_ge(s["bd"], 4)
            nc.scalar.activation(bound[:, 1:2], bound[:, 0:1], ACT.Sqrt, scale=1.02).then_inc(s["bd_sqrt"], 1)
            act.wait_ge(s["plan_ready"], 1)
            n = act.value_load(plan[0:1, 64:65], min_val=1, max_val=T)
            act.sem_inc(s["ex"], 2)
            with act.Fori(0, n) as i:
                for u in range(16):
                    act.wait_ge(s["qk"], i * 16 + u + 1)
                    act.wait_ge(s["pv"], i * 8 + u // 2 + 1)
                    nc.scalar.activation(arenaB[:, u % 4, :], bank[:, 2 * (u % 2):2 * (u % 2) + 2, :].rearrange("p a b -> p (a b)"),
                                         ACT.Exp, scale=SCALE).then_inc(s["ex"], 1)
            for k in range(16):
                act.wait_ge(s["wtb_ps"], k + 1)
                dst = w1T[:, k % 8, :, :] if k < 8 else w2T[:, k - 8, :, :]
                nc.scalar.activation(dst, bank[:, 6 + k % 2, :].rearrange("p (a b) -> p a b", a=FT), ACT.Copy).then_inc(s["wtb_sb"], 1)
                if k == 7:
                    act.wait_ge(s["ln2"], 6)
                    nc.scalar.activation(stat[:, 2, :], stat[:, 1, :], ACT.Sqrt).then_inc(s["sqrt2"], 1)
            act.wait_ge(s["gt"], 2)
            nc.scalar.activation(g[:, 1, :], g[:, 0, :], ACT.Exp).then_inc(s["gtexp"], 1)
            for e in range(E):
                for k in range(2 * FT):
                    c = e * 2 * FT + k
                    act.wait_ge(s["hps"], c + 1)
                    if e >= 2 and k == 0:
                        act.wait_ge(s["yps"], (e - 1) * QT)
                    nc.scalar.activation(hT[:, e % 2, k // 2, 512 * (k % 2):512 * (k % 2) + 512], bank[:, 4 + c % 2, :],
                                         ACT.Gelu_apprx_tanh, bias=b1T[:, k // 2, e:e + 1]).then_inc(s["hact"], 1)

        @block.tensor
        def _(pe):
            mm = nc.tensor.matmul
            pe.wait_ge(s["const"], 12)
            pe.wait_ge(s["w_in"], 64)
            for i in range(4):
                last = nc.tensor.transpose(bank[:, 4, i * P:(i + 1) * P], wraw[:, i, :], ident[:, :])
            last.then_inc(s["wt_ps"], 1)
            pe.wait_ge(s["ln"], 12)
            for t in range(QT):
                last = nc.tensor.transpose(bank[:, t // 4, (t % 4) * P:(t % 4 + 1) * P], xn[:, t, :], ident[:, :])
                if t % 4 == 3:
                    last.then_inc(s["xnT_ps"], 1)
            pe.wait_ge(s["wt_sb"], 1)
            pe.wait_ge(s["row_in"], 80)
            for k in range(2):
                pe.wait_ge(s["xT_sb"], k + 1)
                mm(bank[:, 2 + k, :], wT[:, 0, :], xT[:, 512 * k:512 * k + 512], start=True, stop=False)
                last = mm(bank[:, 2 + k, :], brow[0:1, 0, :], ones[0:1, :], start=False, stop=True)
            last.then_inc(s["q_ps"], 1)
            pe.wait_ge(s["gate_in"], 16)
            pe.wait_ge(s["b1_in"], 16)
            last = nc.tensor.transpose(bank[:, 5, 0:E], gate_raw[:, :], ident[0:E, 0:E])
            for a in range(FT):
                last = nc.tensor.transpose(bank[:, 5, 64 + a * E:64 + (a + 1) * E], b1_raw[:, a * P:(a + 1) * P], ident[0:E, 0:E])
            last.then_inc(s["wt_ps"], 1)
            pe.wait_ge(s["wt_sb"], 3)
            pe.wait_ge(s["hs"], 1)
            for k in range(2):
                pe.wait_ge(s["sqr"], k + 1)
                last = mm(bank[0:H, 6 + k, :], headsel[:, :], squares[:, k, :], start=True, stop=True)
            last.then_inc(s["qn_ps"], 1)
            pe.wait_ge(s["qn"], 1)
            pe.wait_ge(s["q_sb"], 4)
            pe.wait_ge(s["ctx_in"], 16)
            cuts = {t0: k for k, (t0, _) in enumerate(CTX_CUTS)}
            for c in range(CHUNKS + 2):
                if c < CHUNKS:
                    tiles = range(4 * c, min(4 * c + 4, T))
                    if c >= 2:
                        pe.wait_ge(s["cc_sb"], c - 1)
                    for t in tiles:
                        if t in cuts:
                            pe.wait_ge(ctx_in_s[cuts[t]], 16)
                        last = nc.tensor.transpose(bank[:, c % 2, (t - 4 * c) * P:(t - 4 * c + 1) * P], ctx_sb[:, t, :], ident[:, :])
                    last.then_inc(s["cc_ps"], 1)
                if 1 <= c <= CHUNKS:
                    w = min(512, KW - 512 * (c - 1))
                    pe.wait_ge(s["cc_sb"], c)
                    if c >= 3:
                        pe.wait_ge(s["sqr"], c)
                    mm(bank[:, 6 + (c - 1) % 2, 0:w], wT[:, 1, :], ctx_cT[:, (c - 1) % 2, 0:w], start=True, stop=True).then_inc(s["kk_ps"], 1)
                if c >= 2:
                    w = min(512, KW - 512 * (c - 2))
                    pe.wait_ge(s["sqr"], c + 1)
                    if c >= 4:
                        pe.wait_ge(s["kn"], c - 3)
                    mm(bank[0:H, 2 + (c - 2) % 2, 0:w], headsel[:, :], squares[:, (c - 2) % 2, 0:w], start=True, stop=True).then_inc(s["kn_ps"], 1)
            pe.wait_ge(s["sqr"], CHUNKS + 2)
            pe.wait_ge(s["pl_sb"], 1)
            mm(b6[0:T, 0:1], cnt4[:, :], ones[:, 0:1], start=True, stop=True).then_inc(s["pl_ps"], 1)
            pe.wait_ge(s["pl_sb"], 2)
            mm(b6[0:T, 1:2], tri[0:T, 0:T], tcol[0:T, 0:1], start=True, stop=True).then_inc(s["pl_ps"], 1)
            pe.wait_ge(s["pl_sb"], 4)
            mm(b6[0:1, 64:128], iota_p[0:T, :], hot[0:T, :], start=True, stop=True)
            mm(b6[0:1, 128:129], tcol[0:T, 0:1], ones[0:T, 0:1], start=True, stop=True).then_inc(s["pl_ps"], 1)
            pe.wait_ge(s["bd"], 3)
            mm(bank[0:1, 4, 0:H], norms[:, 20:21], ident[0:H, 0:H], start=True, stop=True).then_inc(s["bd_ps"], 1)
            pe.wait_ge(s["plan_ready"], 1)
            mm(bank[:, 7, 0:1], ones[0:1, 0:P], bound[0:1, 3:4], start=True, stop=True).then_inc(s["bd_row"], 1)
            pe.wait_ge(s["plan_ready"], 1)
            pe.wait_ge(s["pl_sb"], 5)
            n = pe.value_load(plan[0:1, 64:65], min_val=1, max_val=T)

            def project(i, cb, ct, ctsb, kv, values):
                pe.wait_ge(cb, i + 1)
                nc.tensor.transpose(b6[:, 0:P], cbuf[:, :], ident[:, :]).then_inc(ct, 1)
                pe.wait_ge(ctsb, i + 1)
                mm(b6[:, P:2 * P], wT[:, 1, :], cT[:, :], start=True, stop=False)
                last = mm(b6[:, P:2 * P], brow[0:1, 1, :], ones[0:1, 0:P], start=False, stop=True)
                if values:
                    mm(b6[:, 2 * P:3 * P], cT[:, :], wT[:, 2, :], start=True, stop=False)
                    last = mm(b6[:, 2 * P:3 * P], ones[0:1, 0:P], brow[0:1, 2, :], start=False, stop=True)
                last.then_inc(kv, 1)

            pe.wait_ge(s["qr"], 16 * NC)
            pe.wait_ge(s["qzero"], 4)
            general = pe.value_load(plan[0:1, 65:66], min_val=0, max_val=1)
            with pe.If(general):
                pe.sem_inc(s["m_ct"], 1)
                pe.sem_inc(s["m_qk"], 1)
                project(0, s["m_cb"], s["m_ct"], s["m_ctsb"], s["m_kv"], False)
                with pe.Fori(0, n) as i:
                    pe.wait_ge(s["m_kc"], i + 2)
                    pe.wait_ge(s["m_mb"], i + 1)
                    for u in range(16):
                        t, hh = u // 2, u % 2
                        pe.wait_ge(s["m_red"], i * 16 + u + 1)
                        for a in range(2):
                            o = bank[:, 2 * hh + a, :]
                            mm(o, nbig[:, :], mbf[:, t, :].rearrange("p (a k) -> p a k", a=1).broadcast_to([P, 4, P]), start=True, stop=False)
                            for b in range(4):
                                h = 8 * hh + 4 * a + b
                                last = mm(o[:, b * P:(b + 1) * P], qS[:, h, t * P:(t + 1) * P], kcur[:, h, :], start=False, stop=(b == 3))
                        last.then_inc(s["m_qk"], 1)
                        if u == 3:
                            pe.wait_ge(s["m_kch"], i * 4 + 4)
                            project(i + 1, s["m_cb"], s["m_ct"], s["m_ctsb"], s["m_kv"], False)
                pe.wait_ge(s["m_fin"], 5)
                pt = bank[:, 0, 0:192].bitcast(BF16)
                for c in range(3):
                    last = nc.tensor.transpose(pt[:, c * P:(c + 1) * P], mparts[:, c, :], identb[:, :])
                last.then_inc(s["m_finT"], 1)
                pe.wait_ge(s["m_kch"], n * 4 + 4)

                pe.wait_ge(s["shift"], 48)
                pe.sem_inc(s["pe_at"], 1)
            pe.sem_inc(s["ct"], 1)
            pe.sem_inc(s["pv"], 2)
            pe.sem_inc(s["mt"], 1)

            def scores(i, u, ui, tile_of, hides):
                pe.wait_ge(s["ex"], i * 16 + ui + 1)
                kk = u // 2
                for a in range(2):
                    h = 4 * (kk // 2) + 2 * (u % 2) + a
                    o, cols = bank[:, 2 * (u % 2) + a, :], slice(512 * (kk % 2), 512 * (kk % 2) + 512)
                    if hides:
                        mm(o, nbig[:, :], maskT[:, bass.ds(tile_of % 2, 1), cols].rearrange("p a q -> p (a q)"), start=True, stop=False)
                    last = mm(o, kcur[:, h, :], qS[:, h, cols], start=not hides, stop=True)
                last.then_inc(s["qk"], 1)

            def mask_count(i):
                pe.wait_ge(s["mc"], i + 1)
                mm(bank[0:1, 7, 0:1], mcount[:, :], ones[:, 0:1], start=True, stop=True).then_inc(s["cm"], 1)

            def values(i, k):
                pe.wait_ge(s["ex"], i * 16 + 2 * k + 4)
                pe.wait_ge(s["ac"], i * 8 + k + 1)
                if k == 0:
                    pe.wait_ge(s["vc"], i + 1)
                for j in range(4):
                    last = mm(bank[32 * j:32 * j + 32, 4 + k % 2, :], vcur[:, 4 * (k // 2) + j, :],
                              arenaB[:, (2 * k + j // 2) % 4, 512 * (j % 2):512 * (j % 2) + 512], start=True, stop=True,
                              tile_position=(0, 32 * j))
                last.then_inc(s["pv"], 1)

            def hides(i):
                return pe.value_load(mixed[0:1, bass.ds(i % 2, 1)], min_val=0, max_val=1)

            def mask_turn(i):
                pe.wait_ge(s["mb"], i + 1)
                for t in range(QT):
                    last = nc.tensor.transpose(maskT_ps[:, t * P:(t + 1) * P], mbf[:, t, :], identb[:, :])
                last.then_inc(s["mt"], 1)

            project(0, s["cb"], s["ct"], s["ctsb"], s["kv"], True)
            mask_turn(0)
            mask_count(0)
            pe.wait_ge(s["kc"], 2)
            pe.wait_ge(s["fl"], 1)
            scores(0, 0, 0, 0, True)
            scores(0, 1, 1, 0, True)
            def seven(i, masked):
                for k in range(7):
                    scores(i, 2 * k + 2, 2 * k + 2, i, masked)
                    scores(i, 2 * k + 3, 2 * k + 3, i, masked)
                    values(i, k)
                    if k == 1:
                        pe.wait_ge(s["kch"], i * 4 + 4)
                        project(i + 1, s["cb"], s["ct"], s["ctsb"], s["kv"], True)
                        mask_turn(i + 1)
                    if k == 3:
                        mask_count(i + 1)

            with pe.Fori(0, n) as i:
                with pe.If(hides(i)):
                    seven(i, True)
                with pe.Else():
                    seven(i, False)
                pe.wait_ge(s["kc"], i + 3)
                pe.wait_ge(s["fl"], i + 2)
                with pe.If(hides(i + 1)):
                    scores(i, 0, 16, i + 1, True)
                    scores(i, 1, 17, i + 1, True)
                with pe.Else():
                    scores(i, 0, 16, i + 1, False)
                    scores(i, 1, 17, i + 1, False)
                values(i, 7)

            pe.wait_ge(s["ac"], n * 8 + 2)
            pe.wait_ge(s["vc"], n + 1)
            pe.wait_ge(s["cs_sb"], 1)
            mm(b6[:, 200:201], csum[:, :], ones[:, 0:1], start=True, stop=True).then_inc(s["cs_ps"], 1)
            pe.wait_ge(s["cs_sb"], 2)
            mm(b6[0:1, 256:384], csT[:, :], wT[:, 2, :], start=True, stop=True).then_inc(s["cs_ps"], 1)
            pe.wait_ge(s["cs_sb"], 3)
            mm(b6[:, 384:512], ones[0:1, 0:P], vsrow[0:1, :], start=True, stop=False)
            mm(b6[:, 384:512], s2row[0:1, :], brow[0:1, 2, :], start=False, stop=True).then_inc(s["cs_ps"], 1)
            pe.wait_ge(s["cs_sb"], 4)

            for hf in range(2):
                for t in range(4):
                    for gg in range(4):
                        q = (4 * hf + t) * P
                        last = nc.tensor.transpose(bank[:, 4 * hf + t, gg * P:(gg + 1) * P], accU[:, gg, q:q + P], ident[:, :])
                last.then_inc(s["u_ps"], 1)
            for t in range(QT):
                pe.wait_ge(s["u_dve"], 5 * (t // 4) + 5)
                last = nc.tensor.transpose(bank[:, t // 4, (t % 4) * P:(t % 4 + 1) * P], ctxq[:, t, :], ident[:, :])
                if t % 4 == 3:
                    last.then_inc(s["cq_ps"], 1)
            def expert_weights():
                pe.wait_ge(s["w1_in"], 16)
                for k in range(16):
                    if k >= 2:
                        pe.wait_ge(s["wtb_sb"], k - 1)
                    if k == 0:
                        pe.wait_ge(s["u_dve"], 10)
                    if k == 8:
                        pe.wait_ge(s["w2_in"], 16)
                    for a in range(FT):
                        src = w1raw[:, a, k, :] if k < 8 else w2raw[:, k - 8, a * P:(a + 1) * P]
                        last = nc.tensor.transpose(bank[:, 6 + k % 2, a * P:(a + 1) * P], src, ident[:, :])
                    last.then_inc(s["wtb_ps"], 1)

            for t in range(QT):
                pe.wait_ge(s["cq_sb"], t // 4 + 1)
                o = bank[:, 2 + t // 4, (t % 4) * P:(t % 4 + 1) * P]
                mm(o, ctxqT[:, t * P:(t + 1) * P], wT[:, 3, :], start=True, stop=False)
                last = mm(o, ones[0:1, 0:P], brow[0:1, 3, :], start=False, stop=True)
            last.then_inc(s["at_ps"], 1)
            expert_weights()
            pe.wait_ge(s["ln2"], 12)
            for t in range(QT):
                last = nc.tensor.transpose(bank[:, t // 4, (t % 4) * P:(t % 4 + 1) * P], xn2[:, t, :], ident[:, :])
                if t % 4 == 3:
                    last.then_inc(s["x2T_ps"], 1)
            pe.wait_ge(s["x2T_sb"], 2)
            for t in range(QT):
                last = mm(bank[:, 2, t * E:(t + 1) * E], x2T[:, t * P:(t + 1) * P], gateT[:, :], start=True, stop=True)
            last.then_inc(s["lg"], 1)

            def up(e):
                for k in range(2 * FT):
                    c = e * 2 * FT + k
                    if c >= 2:
                        pe.wait_ge(s["hact"], c - 1)
                    mm(bank[:, 4 + c % 2, :], w1T[:, e, k // 2, :], x2T[:, 512 * (k % 2):512 * (k % 2) + 512],
                       start=True, stop=True).then_inc(s["hps"], 1)

            def down(e):
                pe.wait_ge(s["hact"], (e + 1) * 2 * FT)
                for t in range(QT):
                    c = e * QT + t
                    if c >= 2:
                        pe.wait_ge(s["yacc"], c)
                    for a in range(FT):
                        last = mm(bank[:, 6 + t % 2, 0:P], hT[:, e % 2, a, t * P:(t + 1) * P], w2T[:, e, a, :],
                                  start=(a == 0), stop=(a == FT - 1))
                    last.then_inc(s["yps"], 1)

            up(0)
            pe.wait_ge(s["gt"], GATE_STEPS)
            pe.wait_ge(s["b2_in"], 16)
            for t in range(QT):
                last = nc.tensor.transpose(bank[0:E, t // 4, (t % 4) * P:(t % 4 + 1) * P], g[:, 9, t * E:(t + 1) * E], ident[:, :])
                if t % 4 == 3:
                    last.then_inc(s["gT_ps"], 1)
            pe.wait_ge(s["gT_sb"], 2)
            for t in range(QT):
                last = mm(bank[:, 2 + t // 4, (t % 4) * P:(t % 4 + 1) * P], epi_e[:, t * P:(t + 1) * P], b2_sb[:, :], start=True, stop=True)
            last.then_inc(s["b2ps"], 1)
            for e in range(E):
                if e + 1 < E:
                    up(e + 1)
                down(e)


_INS = ['x', 'ctx_1024', 'mask_BxSxS2_bk1', 'L0_xattn_Wq', 'L0_xattn_bq', 'L0_xattn_Wk', 'L0_xattn_bk', 'L0_xattn_Wv',
        'L0_xattn_bv', 'L0_xattn_Wo', 'L0_xattn_bo', 'L0_ffn_gate_w', 'L0_ffn_w1', 'L0_ffn_b1', 'L0_ffn_w2', 'L0_ffn_b2']


def kernel(**inputs):
    import numpy as _np
    import concourse.bacc as _bacc
    from concourse import mybir as _mybir
    from concourse.bass_utils import run_bass_kernel_spmd as _run

    nc = _bacc.Bacc("TRN2", target_bir_lowering=False, num_devices=1)
    arrays, args = {}, []
    for name in _INS:
        a = _np.ascontiguousarray(inputs[name])
        arrays[f"in_{name}_dram"] = a
        args.append(nc.dram_tensor(f"in_{name}_dram", a.shape, _mybir.dt.from_np(a.dtype), kind="ExternalInput").ap())
    args.append(nc.dram_tensor("out_0_dram", (1, S, D), F32, kind="ExternalOutput").ap())
    build(nc, *args)
    r = _run(nc, [arrays], core_ids=[0])
    return r.results[0]["out_0_dram"]
```

```python
import concourse.bass as bass
from concourse import mybir
from contextlib import ExitStack

F32 = mybir.dt.float32
BF16 = mybir.dt.bfloat16
U8 = mybir.dt.uint8
U16 = mybir.dt.uint16
I32 = mybir.dt.int32
ACT = mybir.ActivationFunctionType
ALU = mybir.AluOpType
AX = mybir.AxisListType

P = 128
S, D, H = 1024, 128, 16
HD = D // H
S2 = 6404
E, F = 8, 512
QT = S // P
FT = F // P
T = -(-S2 // P)
PAD = T * P - S2
KW = T * P
SCALE = float(HD) ** -0.5
BIG = 2.0 ** 100
EPS = 1e-5
FOLD_STEPS = 7
GATE_STEPS = 18
NC = 9
CHUNKS = -(-T // 4)
BF16_ONES = 1.0 + 0x3F80 / 2.0 ** 23
BOUND = 40.0
CTX_CUTS = [(1, 12), (12, 24), (24, 36), (36, T)]
SHIFT_ROW = 96


def build(nc, x, ctx_in, mask, Wq, bq, Wk, bk, Wv, bv, Wo, bo, gate_w, w1, b1, w2, b2, out):
    with ExitStack() as es:
        def sb(name, shape, dt):
            return es.enter_context(nc.sbuf_tensor(name, shape, dt))

        def sem(name):
            return es.enter_context(nc.semaphore(name))

        kparts_dram = nc.dram_tensor("kparts_dram", (3, P, P), BF16, kind="Internal").ap()
        qparts_dram = nc.dram_tensor("qparts_dram", (3, P, S), BF16, kind="Internal").ap()

        mask_u8 = sb("mask_u8", [P, QT, KW], U8)
        ctx_sb = sb("ctx_sb", [P, T, D], F32)
        x_sb = sb("x_sb", [P, QT, D], F32)
        arenaA = sb("arenaA", [P, 4096], F32)
        arenaB = sb("arenaB", [P, 4, 1024], F32)
        qS = sb("qS", [P, H, S], BF16)
        arenaC = sb("arenaC", [P, 1664], F32)
        wT = sb("wT", [P, 4, D], F32)
        wk_turned = sb("wk_turned", [P, D], F32)
        bk_turned = sb("bk_turned", [1, D], F32)
        gateT = sb("gateT", [P, E], F32)
        b1T = sb("b1T", [P, FT, E], F32)
        b2_sb = sb("b2_sb", [E, D], F32)
        w1T = sb("w1T", [P, E, FT, P], F32)
        w2T = sb("w2T", [P, E, FT, D], F32)
        brow = sb("brow", [1, 4, D], F32)
        ones = sb("ones", [P, 512], F32)
        ident = sb("ident", [P, P], F32)
        identb = sb("identb", [P, P], BF16)
        nbig = sb("nbig", [P, P], BF16)
        maskT = sb("maskT", [P, 2, S], BF16)
        stat = sb("stat", [P, 5, QT], F32)
        keys = sb("keys", [P, 2, H, P], BF16)
        vcur = sb("vcur", [P, H, 32], F32)
        cnt4 = sb("cnt4", [P, 2, T], F32)
        tcol = sb("tcol", [64, 5], F32)
        headsel = sb("headsel", [P, H], BF16)
        bkcol = sb("bkcol", [P, 1], F32)
        norms = sb("norms", [H, 4], F32)
        shift_fill = sb("shift_fill", [P, 2 * H], BF16)
        bound = sb("bound", [1, 4], F32)
        tri = sb("tri", [64, 64], F32)
        iota_s = sb("iota_s", [64, 64], F32)
        iota_p = sb("iota_p", [64, 1], F32)
        hot = sb("hot", [64, 64], F32)
        plan = sb("plan", [1, 72], I32)
        iota_e = sb("iota_e", [P, QT * E], F32)

        peak = maskT[:, :, :].rearrange("p a q -> p (a q)").bitcast(F32)
        tmax = peak[:, 0:128].rearrange("p (h t) -> p h t", t=QT)
        rmax = peak[:, 768:896].rearrange("p (h t) -> p h t", t=QT)
        mres = peak[:, 128:384].rearrange("p (a k) -> p a k", a=2)
        mparts = peak[:, 384:576].bitcast(BF16).rearrange("p (c k) -> p c k", c=3)
        mpT = peak[:, 576:768].bitcast(BF16).rearrange("p (c k) -> p c k", c=3)

        xn = arenaA[:, 0:1024].rearrange("p (t d) -> p t d", d=D)
        sq = arenaA[:, 1024:2048].rearrange("p (t d) -> p t d", d=D)
        qres = arenaA[:, 1024:2048]
        qparts = arenaA[:, 2048:3584].bitcast(BF16).rearrange("p (c q) -> p c q", c=3)
        ctx_cT = w2T[:, :, :, :].rearrange("p e a d -> p (e a d)")[:, 0:1024].rearrange("p (b k) -> p b k", b=2)
        early = w2T[:, :, :, :].rearrange("p e a d -> p (e a d)")
        xT = early[:, 0:1024]
        wraw = early[:, 1024:1536].rearrange("p (a d) -> p a d", a=4)
        gate_raw = early[0:E, 1536:1664]
        b1_raw = early[0:E, 1664:2176]
        probs = [arenaB[:, k, :] for k in range(4)] + [early[:, 1024 * k:1024 * k + 1024] for k in range(4)]
        or_acc = w1T[:, :, :, :].rearrange("p e a d -> p (e a d)")[:, 0:KW // 4].bitcast(I32)
        fold = w1T[:, :, :, :].rearrange("p e a d -> p (e a d)")[:, KW // 4:KW // 4 + T // 3 * D]
        csum = fold[:, 0:D]
        and_acc = arenaC[:, 0:KW // 4].bitcast(I32)
        cT = arenaC[:, 512:640]
        vsumB = arenaC[:, 1473:1601]
        g1 = arenaC[:, 1601:1649].rearrange("p (a t) -> p a t", a=6)
        vsrow = arenaC[0:1, 1344:1472]
        csT = arenaC[:, 1472:1473]
        cbuf = arenaC[:, 1024:1152]
        kparts = arenaC[:, 1152:1344].bitcast(BF16).rearrange("p (c k) -> p c k", c=3)
        kres = arenaC[:, 640:768].rearrange("p (a k) -> p a k", a=1)
        s2row = arenaC[0:1, 768:896]
        vnext = arenaC[:, 896:1024]
        mbf = arenaC[:, 0:512].bitcast(BF16).rearrange("p (t k) -> p t k", t=QT)
        accU = arenaA[:, :].rearrange("p (g q) -> p g q", g=4)
        masks_f32 = mask_u8[:, :, :].rearrange("p t k -> p (t k)").bitcast(F32)
        w1raw = masks_f32[:, 8192:12288].rearrange("p (a e d) -> p a e d", a=4, e=E)
        w2raw = masks_f32[:, 4096:8192].rearrange("p (e f) -> p e f", e=E)
        after = ctx_sb[:, :, :].rearrange("p t d -> p (t d)")
        x2 = after[:, 0:1024].rearrange("p (t d) -> p t d", d=D)
        xn2 = after[:, 1024:2048].rearrange("p (t d) -> p t d", d=D)
        x2T = after[:, 2048:3072]
        ctxq = after[:, 3072:4096].rearrange("p (t d) -> p t d", d=D)
        ctxqT = after[:, 4096:5120]
        sq2 = after[:, 5120:6144].rearrange("p (t d) -> p t d", d=D)
        g = after[:, 5120:5888].rearrange("p (a b) -> p a b", a=12)
        epi_e = after[0:E, 3072:4096]
        nmax = early[:, 2688:2720].rearrange("p (a h) -> p a h", a=2)
        squares = early[:, 2176:2688].bitcast(BF16).rearrange("p (b k) -> p b k", b=2)
        hT = masks_f32[:, 0:8192].rearrange(
            "p (b t q) -> p b t q", b=2, t=FT)
        maskw = mask_u8[:, :, :].bitcast(I32)

        bank = es.enter_context(nc.psum_tensor("bank", [P, 8, 512], F32))
        maskT_ps = bank[:, 7, :].bitcast(BF16)
        b6 = bank[:, 6, :]
        sizes = bank[:, 4:6, :].rearrange("p a (t h) -> p (a t) h", h=H)

        names = ("x_in w_in row_in gate_in b1_in b2_in w1_in w2_in ctx_in ctxpad pad const ln sqrt xnT_ps xT_sb "
                 "q_ps q_sb qw qr qzero wt_ps wt_sb wtb_ps wtb_sb and_ cs_ps cs_sb pl_ps pl_sb plan_ready m_cb "
                 "m_ct m_ctsb m_kv m_kch m_kw m_kr m_mb m_qk m_red m_max m_fin m_finT m_finsb shift cb ct ctsb kv "
                 "kch kw kr vc mb mt mc vn fold or_ qk ex pv ac u_ps u_dve cq_ps cq_sb at_ps x2s ln2 sqrt2 x2T_ps "
                 "x2T_sb lg gt gtexp gT_ps gT_sb hps hact yps yacc b2ps outs vinit sp_at pool_at dve_at pe_at hs "
                 "qn_ps kn_ps bd bd_ps bd_sqrt bd_row kones sqr cc_ps cc_sb kk_ps wk_sb s2 bias kzero vzero "
                 "kshift").split()
        s = {n: sem(n) for n in names}
        ctx_in_s = [sem(f"ctx_in{k}") for k in range(len(CTX_CUTS))]
        mask_in = [sem(f"mask_in{t}") for t in range(QT)]

        block = es.enter_context(nc.Block())

        @block.sync
        def _(sp):
            sp.dma_start(x_sb[:, :, :], x.rearrange("a (p t) d -> p (a t) d", t=QT)).then_inc(s["x_in"], 16)
            for i, w in enumerate((Wq, Wk, Wv, Wo)):
                sp.dma_start(wraw[:, i, :], w).then_inc(s["w_in"], 16)
            sp.dma_start(bkcol[:, :], bk.rearrange("(n a) -> n a", a=1)).then_inc(s["row_in"], 16)
            for i, b in enumerate((bq, bk, bv, bo)):
                sp.dma_start(brow[0:1, i, :], b.rearrange("(a n) -> a n", a=1)).then_inc(s["row_in"], 16)
            c = ctx_in[0, P - PAD:S2, :].rearrange("(t p) d -> p t d", p=P)
            for k, (t0, t1) in enumerate(CTX_CUTS):
                sp.dma_start(ctx_sb[:, t0:t1, :], c[:, t0 - 1:t1 - 1, :]).then_inc(ctx_in_s[k], 16)
            m = mask.rearrange("a (p t) k -> p (a t) k", t=QT)
            for t in range(QT):
                sp.dma_start(mask_u8[:, t, PAD:KW], m[:, t, :]).then_inc(mask_in[t], 16)
            sp.wait_ge(s["q_sb"], 4)
            sp.dma_start(qparts_dram.rearrange("c p q -> p c q"), qparts[:, :, :]).then_inc(s["qw"], 16)
            sp.wait_ge(s["qw"], 16)
            sp.wait_ge(s["qzero"], 2)
            for c in range(NC):
                sp.dma_start(qS[c * HD:(c + 1) * HD, :, :],
                             qparts_dram[c // 3, :, :].rearrange("(h d) q -> d h q", d=HD)).then_inc(s["qr"], 16)

            def key_rows(i, chain, written, read, used, per_tile):
                sp.wait_ge(chain, i * 4 + 4)
                sp.dma_start(kparts_dram.rearrange("c p k -> p c k"), kparts[:, :, :]).then_inc(written, 16)
                sp.wait_ge(written, i * 16 + 16)
                sp.sem_inc(s["sp_at"], 1)
                sp.wait_ge(used, i * per_tile + 1)
                sp.sem_inc(s["sp_at"], 1)
                for c in range(3):
                    sp.dma_start(keys[c * 3 * HD:(c + 1) * 3 * HD, bass.ds(i % 2, 1), :, :].rearrange("p a h k -> p (a h k)"),
                                 kparts_dram.rearrange("c (d h) k -> (c d) (h k)", h=H)).then_inc(read, 16)

            sp.wait_ge(s["plan_ready"], 1)
            n = sp.value_load(plan[0:1, 64:65], min_val=1, max_val=T)
            partial = sp.value_load(plan[0:1, 66:67], min_val=0, max_val=T)
            sp.wait_ge(s["kzero"], 1)
            sp.wait_ge(s["bias"], 1)
            sp.dma_start(keys[SHIFT_ROW:SHIFT_ROW + 1, :, :, :].rearrange("p b h k -> p (b h k)").rearrange("a (p k) -> a p k", p=P), shift_fill[:, :]).then_inc(s["kshift"], 16)
            general = sp.value_load(plan[0:1, 65:66], min_val=0, max_val=1)
            with sp.If(general):
                with sp.Fori(0, n + 1) as i:
                    key_rows(i, s["m_kch"], s["m_kw"], s["m_kr"], s["m_qk"], 16)
                sp.wait_ge(s["m_kr"], n * 48 + 48)
                sp.sem_inc(s["sp_at"], 1)
                for c in range(3):
                    sp.wait_ge(s["m_finsb"], 1)
                    sp.dma_start(qS[SHIFT_ROW + c:SHIFT_ROW + 1 + c, :, :].rearrange("a h (t q) -> a (h t) q", q=P),
                                 mpT[:, c, :]).then_inc(s["shift"], 16)
            with sp.Fori(0, n + 1) as i:
                key_rows(i, s["kch"], s["kw"], s["kr"], s["qk"], 16)
            sp.wait_ge(s["mb"], partial + 1)
            sp.sem_inc(s["sp_at"], 1)
            sp.dma_start(w1raw, w1.rearrange("(a p) e d -> p a e d", p=P)).then_inc(s["w1_in"], 16)
            sp.dma_start(w2raw, w2).then_inc(s["w2_in"], 16)
            sp.wait_ge(s["yacc"], E * QT + 1)
            sp.dma_start(out.rearrange("a (p t) d -> p (a t) d", t=QT), x2).then_inc(s["outs"], 16)
            sp.wait_ge(s["outs"], 16)

        @block.gpsimd
        def _(pool):
            pool.dma_start(gate_raw[:, :], gate_w).then_inc(s["gate_in"], 16)
            pool.dma_start(b1_raw[:, :], b1).then_inc(s["b1_in"], 16)
            pool.dma_start(b2_sb[:, :], b2).then_inc(s["b2_in"], 16)
            nc.gpsimd.memset(ident[:, :], 0.0).then_inc(s["const"], 1)
            pool.wait_ge(s["const"], 1)
            nc.gpsimd.affine_select(out=ident[:, :], in_=ident[:, :], compare_op=ALU.not_equal, fill=1.0,
                                    base=0, pattern=[[-1, P]], channel_multiplier=1).then_inc(s["const"], 1)
            nc.gpsimd.memset(ones[:, :], 1.0).then_inc(s["const"], 1)
            pool.wait_ge(s["const"], 3)
            nc.gpsimd.tensor_copy(identb[:, :], ident[:, :]).then_inc(s["const"], 1)
            nc.gpsimd.memset(nbig[:, :], 0.0).then_inc(s["const"], 1)
            nc.gpsimd.memset(tri[:, :], 1.0).then_inc(s["const"], 1)
            pool.wait_ge(s["const"], 6)
            nc.gpsimd.affine_select(out=nbig[:, :], in_=nbig[:, :], compare_op=ALU.not_equal, fill=-BIG,
                                    base=0, pattern=[[-1, P]], channel_multiplier=1).then_inc(s["const"], 1)
            nc.gpsimd.affine_select(out=tri[:, :], in_=tri[:, :], compare_op=ALU.is_gt, fill=0.0,
                                    base=0, pattern=[[1, 64]], channel_multiplier=-1).then_inc(s["const"], 1)
            nc.gpsimd.iota(iota_s[:, :], [[1, 64]], base=0, channel_multiplier=0,
                           allow_small_or_imprecise_dtypes=True).then_inc(s["const"], 1)
            nc.gpsimd.iota(iota_p[:, :], [[0, 1]], base=0, channel_multiplier=1,
                           allow_small_or_imprecise_dtypes=True).then_inc(s["const"], 1)
            nc.gpsimd.iota(iota_e[:, :], [[0, QT], [1, E]], base=0, channel_multiplier=0,
                           allow_small_or_imprecise_dtypes=True).then_inc(s["const"], 1)
            nc.gpsimd.memset(mask_u8[:, :, 0:PAD], 1).then_inc(s["pad"], 1)
            nc.gpsimd.memset(ctx_sb[:, 0, :], 0.0).then_inc(s["ctxpad"], 1)
            pool.wait_ge(s["ctxpad"], 1)
            pool.dma_start(ctx_sb[PAD:P, 0, :], ctx_in[0, 0:P - PAD, :]).then_inc(s["ctx_in"], 16)
            nc.gpsimd.memset(qS[64:SHIFT_ROW, :, :].bitcast(F32), 0.0).then_inc(s["qzero"], 1)
            nc.gpsimd.memset(qS[SHIFT_ROW:P, :, :].bitcast(F32), BF16_ONES).then_inc(s["qzero"], 1)
            pool.wait_ge(s["qzero"], 2)
            nc.gpsimd.memset(keys[64:P, :, :, :].bitcast(F32), 0.0).then_inc(s["kzero"], 1)
            pool.wait_ge(s["kzero"], 1)
            nc.gpsimd.memset(vcur[:, :, :], 0.0).then_inc(s["vzero"], 1)
            pool.wait_ge(s["vzero"], 1)
            nc.gpsimd.memset(vcur[:, :, HD:HD + 1], 1.0).then_inc(s["vinit"], 1)

            for k in range(len(CTX_CUTS)):
                pool.wait_ge(ctx_in_s[k], 16)
            pool.wait_ge(s["ctx_in"], 16)
            cflat = ctx_sb[:, :, :].rearrange("p t d -> p (t d)")
            third = T // 3 * D
            nc.gpsimd.tensor_tensor(fold, cflat[:, 0:third], cflat[:, third:2 * third], ALU.add).then_inc(s["fold"], 1)
            pool.wait_ge(s["fold"], 1)
            nc.gpsimd.tensor_tensor(fold, fold, cflat[:, 2 * third:3 * third], ALU.add).then_inc(s["fold"], 1)
            w, k = T // 3, 2
            while w > 1:
                pool.wait_ge(s["fold"], k)
                if w % 2:
                    nc.gpsimd.tensor_tensor(fold[:, 0:D], fold[:, 0:D], fold[:, (w - 1) * D:w * D], ALU.add).then_inc(s["fold"], 1)
                    w, k = w - 1, k + 1
                    pool.wait_ge(s["fold"], k)
                w //= 2
                last = nc.gpsimd.tensor_tensor(csum[:, :] if w == 1 else fold[:, 0:w * D], fold[:, 0:w * D], fold[:, w * D:2 * w * D], ALU.add)
                k += 1
                last.then_inc(s["fold"], 1)
            assert k == FOLD_STEPS
            pool.wait_ge(s["qw"], 16)
            nc.gpsimd.memset(arenaA[:, :], 0.0).then_inc(s["ac"], 1)
            pool.wait_ge(s["plan_ready"], 1)
            nc.gpsimd.memset(s2row[:, :], float(S2)).then_inc(s["s2"], 1)
            n = pool.value_load(plan[0:1, 64:65], min_val=1, max_val=T)

            def tile_in(i, cb, ct, mb, mask_used, per_tile, first):
                tile = pool.value_load(plan[0:1, bass.ds(i, 1)], min_val=0, max_val=T - 1)
                pool.wait_ge(ct, i + 1)
                nc.gpsimd.tensor_copy(cbuf[:, :], ctx_sb[:, bass.ds(tile, 1), :].rearrange("p a d -> p (a d)")).then_inc(cb, 1)
                if mb is None:
                    return
                pool.wait_ge(mask_used, i * per_tile + first)
                nc.gpsimd.tensor_copy(mbf[:, :, :], mask_u8[:, :, bass.ds(tile * P, P)]).then_inc(mb, 1)

            general = pool.value_load(plan[0:1, 65:66], min_val=0, max_val=1)
            with pool.If(general):
                with pool.Fori(0, n + 1) as i:
                    tile_in(i, s["m_cb"], s["m_ct"], s["m_mb"], s["m_qk"], 16, 17)
                pool.wait_ge(s["m_ct"], n + 2)
                pool.sem_inc(s["pool_at"], 1)
                pool.wait_ge(s["m_mb"], n + 1)
                pool.sem_inc(s["pool_at"], 1)
            with pool.Fori(0, n + 1) as i:
                tile_in(i, s["cb"], s["ct"], None, None, 0, 0)

        def layer_norm(dve, xin, xout, scratch, done, sqrt_done):
            c = [0]

            def step(ins):
                c[0] += 1
                ins.then_inc(done, 1)
                dve.wait_ge(done, c[0])

            mean, var, root, inv, t1 = (stat[:, k, :] for k in range(5))
            step(nc.vector.tensor_reduce(mean, xin, axis=AX.X, op=ALU.add))
            step(nc.vector.tensor_scalar(mean, mean, 1.0 / D, None, ALU.mult))
            step(nc.vector.tensor_tensor(xout, xin, mean.rearrange("p (t a) -> p t a", a=1).broadcast_to([P, QT, D]), ALU.subtract))
            step(nc.vector.tensor_tensor(scratch, xout, xout, ALU.mult))
            step(nc.vector.tensor_reduce(var, scratch, axis=AX.X, op=ALU.add))
            step(nc.vector.tensor_scalar(var, var, 1.0 / D, EPS, ALU.mult, ALU.add))
            dve.wait_ge(sqrt_done, 1)
            step(nc.vector.reciprocal(inv, root))
            step(nc.vector.tensor_tensor(t1, var, inv, ALU.mult))
            step(nc.vector.tensor_tensor(t1, t1, root, ALU.add))
            step(nc.vector.tensor_scalar(t1, t1, 0.5, None, ALU.mult))
            step(nc.vector.reciprocal(inv, t1))
            nc.vector.tensor_tensor(xout, xout, inv.rearrange("p (t a) -> p t a", a=1).broadcast_to([P, QT, D]), ALU.mult).then_inc(done, 1)

        def parts3(dve, dst, src, res, chain, base):
            nc.vector.tensor_copy(dst[0], src).then_inc(chain, 1)
            dve.wait_ge(chain, base + 1)
            nc.vector.tensor_tensor(res[0], src, dst[0], ALU.subtract).then_inc(chain, 1)
            dve.wait_ge(chain, base + 2)
            nc.vector.tensor_copy(dst[1], res[0]).then_inc(chain, 1)
            dve.wait_ge(chain, base + 3)
            nc.vector.tensor_tensor(dst[2], res[0], dst[1], ALU.subtract).then_inc(chain, 1)

        @block.vector
        def _(dve):
            dve.wait_ge(s["x_in"], 16)
            layer_norm(dve, x_sb[:, :, :], xn, sq, s["ln"], s["sqrt"])
            for k in range(2):
                dve.wait_ge(s["xnT_ps"], k + 1)
                nc.vector.tensor_copy(xT[:, 512 * k:512 * k + 512], bank[:, k, :]).then_inc(s["xT_sb"], 1)
            dve.wait_ge(s["q_ps"], 1)
            qp = bank[:, 2:4, :].rearrange("p a b -> p (a b)")
            parts3(dve, [qparts[:, k, :] for k in range(3)], qp, [qres], s["q_sb"], 0)

            dve.wait_ge(s["const"], 11)
            nc.vector.tensor_reduce(headsel[:, :], identb[:, :].rearrange("p (h d) -> p h d", d=HD), axis=AX.X, op=ALU.max).then_inc(s["hs"], 1)
            dve.wait_ge(s["pad"], 1)
            dve.wait_ge(mask_in[0], 16)
            for t in range(1, QT):
                dve.wait_ge(mask_in[t], 16)
                if t > 1:
                    dve.wait_ge(s["and_"], t - 1)
                nc.vector.scalar_tensor_tensor(and_acc[:, :], maskw[:, 0, :] if t == 1 else and_acc[:, :], 1, maskw[:, t, :],
                                               ALU.logical_shift_left, ALU.bitwise_or).then_inc(s["and_"], 1)
            c = QT - 1
            w = P // 4
            av = and_acc[:, :].rearrange("p (t w) -> p t w", w=w)
            ov = or_acc.rearrange("p (t w) -> p t w", w=w)
            dve.wait_ge(s["and_"], c)
            nc.vector.tensor_tensor(ov[:, :, 0:w // 2], av[:, :, 0:w // 2], av[:, :, w // 2:w], ALU.bitwise_or).then_inc(s["or_"], 1)
            dve.wait_ge(s["or_"], 1)
            nc.vector.tensor_tensor(av[:, :, 0:w // 2], av[:, :, 0:w // 2], av[:, :, w // 2:w], ALU.bitwise_and).then_inc(s["and_"], 1)
            c, w, d = c + 1, w // 2, 1
            while w > 1:
                w //= 2
                dve.wait_ge(s["and_"], c)
                nc.vector.tensor_tensor(av[:, :, 0:w], av[:, :, 0:w], av[:, :, w:2 * w], ALU.bitwise_and).then_inc(s["and_"], 1)
                dve.wait_ge(s["or_"], d)
                nc.vector.tensor_tensor(ov[:, :, 0:w], ov[:, :, 0:w], ov[:, :, w:2 * w], ALU.bitwise_or).then_inc(s["or_"], 1)
                c, d = c + 1, d + 1
            dve.wait_ge(s["and_"], c)
            dve.wait_ge(s["or_"], d)
            ab = and_acc[:, :].bitcast(U8).rearrange("p (t b) -> p t b", b=P)[:, :, 0:4]
            ob = or_acc.bitcast(U8).rearrange("p (t b) -> p t b", b=P)[:, :, 0:4]
            nc.vector.tensor_reduce(cnt4[:, 0, :], ab, axis=AX.X, op=ALU.add)
            nc.vector.tensor_reduce(cnt4[:, 1, :], ob, axis=AX.X, op=ALU.add).then_inc(s["pl_sb"], 1)
            dve.wait_ge(s["kn_ps"], CHUNKS)
            nc.vector.tensor_reduce(nmax[:, 0, :], sizes[:, T:T + QT, :].rearrange("p t h -> p h t"), axis=AX.X, op=ALU.max).then_inc(s["bd"], 1)
            nc.vector.tensor_reduce(nmax[:, 1, :], sizes[:, 0:T, :].rearrange("p t h -> p h t"), axis=AX.X, op=ALU.max).then_inc(s["bd"], 1)
            dve.wait_ge(s["pl_ps"], 1)
            nc.vector.tensor_scalar(tcol[0:T, 0:1], b6[0:T, 0:1], 255.0 * 4 * P - 0.5, None, ALU.is_lt)
            nc.vector.tensor_scalar(tcol[0:T, 1:2], b6[0:T, 1:2], 0.5, None, ALU.is_lt).then_inc(s["pl_sb"], 1)
            dve.wait_ge(s["pl_sb"], 2)
            nc.vector.tensor_tensor(tcol[0:T, 2:3], tcol[0:T, 0:1], tcol[0:T, 1:2], ALU.subtract).then_inc(s["pl_sb"], 1)
            dve.wait_ge(s["bd_ps"], 1)
            nc.vector.tensor_reduce(norms[:, 0:2], bank[0:H, 2, 0:2 * P].rearrange("p (a k) -> p a k", a=2), axis=AX.X, op=ALU.max).then_inc(s["bd"], 1)
            dve.wait_ge(s["bd"], 3)
            nc.vector.tensor_tensor(norms[:, 2:3], norms[:, 0:1], norms[:, 1:2], ALU.mult).then_inc(s["bd"], 1)
            dve.wait_ge(s["pl_ps"], 2)
            nc.vector.tensor_tensor(tcol[0:T, 3:4], b6[0:T, 4:5], tcol[0:T, 1:2], ALU.mult).then_inc(s["pl_sb"], 1)
            dve.wait_ge(s["pl_sb"], 4)
            nc.vector.scalar_tensor_tensor(tcol[0:T, 4:5], b6[0:T, 3:4], tcol[0:T, 2:3], tcol[0:T, 3:4], ALU.mult, ALU.add).then_inc(s["pl_sb"], 1)
            dve.wait_ge(s["pl_sb"], 5)
            nc.vector.tensor_scalar(hot[0:T, :], iota_s[0:T, :], tcol[0:T, 4:5], tcol[0:T, 0:1], ALU.is_equal, ALU.mult).then_inc(s["pl_sb"], 1)
            dve.wait_ge(s["bd_ps"], 2)
            nc.vector.tensor_reduce(bound[:, 0:1], bank[0:1, 4, 0:H], axis=AX.X, op=ALU.max).then_inc(s["bd"], 1)
            dve.wait_ge(s["pl_ps"], 3)
            nc.vector.tensor_copy(plan[0:1, 0:64], b6[0:1, 64:128])
            nc.vector.tensor_copy(plan[0:1, 66:67], b6[0:1, 129:130])
            nc.vector.tensor_scalar(plan[0:1, 64:65], b6[0:1, 128:129], 1.0, None, ALU.max).then_inc(s["pl_sb"], 1)
            dve.wait_ge(s["bd_sqrt"], 1)
            nc.vector.tensor_scalar(bound[:, 2:3], bound[:, 1:2], BOUND / SCALE, None, ALU.is_le).then_inc(s["bd"], 1)
            dve.wait_ge(s["bd"], 6)
            nc.vector.tensor_scalar(plan[0:1, 65:66], bound[:, 2:3], -1.0, 1.0, ALU.mult, ALU.add).then_inc(s["bd"], 1)
            nc.vector.scalar_tensor_tensor(bound[:, 3:4], bound[:, 1:2], -1.0, bound[:, 2:3], ALU.mult, ALU.mult).then_inc(s["plan_ready"], 1)

            dve.wait_ge(s["plan_ready"], 1)
            dve.wait_ge(s["bd_row"], 1)
            nc.vector.tensor_copy(shift_fill[:, :], bank[:, 4, 64:65].broadcast_to([P, 2 * H])).then_inc(s["bias"], 1)
            n = dve.value_load(plan[0:1, 64:65], min_val=1, max_val=T)
            def turned(i, ct, ctsb):
                dve.wait_ge(ct, i + 2)
                nc.vector.tensor_copy(cT[:, :], b6[:, 0:P]).then_inc(ctsb, 1)

            def key_parts(i, kv, kch):
                dve.wait_ge(kv, i + 1)
                parts3(dve, [kparts[:, k, :] for k in range(3)], b6[:, P:2 * P], [kres[:, 0, :]], kch, i * 4)

            general = dve.value_load(plan[0:1, 65:66], min_val=0, max_val=1)
            with dve.If(general):
                nc.vector.memset(rmax[:, :, :], -4.0 * BIG).then_inc(s["m_max"], 1)

                dve.sem_inc(s["m_red"], 2)

                def key_parts_max(i):
                    turned(i, s["m_ct"], s["m_ctsb"])
                    key_parts(i, s["m_kv"], s["m_kch"])

                key_parts_max(0)
                with dve.Fori(0, n) as i:
                    for u in range(16):
                        t, hh = u // 2, u % 2
                        dve.wait_ge(s["m_qk"], i * 16 + u + 18)
                        if u == 0:
                            dve.wait_ge(s["m_max"], i + 1)
                        nc.vector.tensor_reduce(tmax[:, 8 * hh:8 * hh + 8, t], bank[:, 2 * hh:2 * hh + 2, :].rearrange("p a (h k) -> p (a h) k", k=P),
                                                axis=AX.X, op=ALU.max).then_inc(s["m_red"], 1)
                        if u == 3:
                            dve.wait_ge(s["m_kw"], i * 16 + 16)
                            key_parts_max(i + 1)
                    dve.wait_ge(s["m_red"], i * 16 + 18)
                    nc.vector.tensor_tensor(rmax[:, :, :], rmax[:, :, :], tmax[:, :, :], ALU.max).then_inc(s["m_max"], 1)
                dve.wait_ge(s["m_max"], n + 1)
                m2 = rmax[:, :, :].rearrange("p h t -> p (h t)")
                nc.vector.tensor_scalar(mres[:, 0, :], m2, -BIG / 4, -1.0, ALU.max, ALU.mult).then_inc(s["m_fin"], 1)
                dve.wait_ge(s["m_fin"], 1)
                parts3(dve, [mparts[:, k, :] for k in range(3)], mres[:, 0, :], [mres[:, 1, :]], s["m_fin"], 1)
                dve.wait_ge(s["m_finT"], 1)
                nc.vector.tensor_copy(mpT[:, :, :], bank[:, 0, 0:192].bitcast(BF16).rearrange("p (c q) -> p c q", c=3)).then_inc(s["m_finsb"], 1)
                dve.wait_ge(s["m_kr"], n * 48 + 48)
                dve.wait_ge(s["shift"], 48)
                dve.wait_ge(s["kshift"], 16)
                nc.vector.memset(keys[SHIFT_ROW:SHIFT_ROW + 3, :, :, :], 1.0).then_inc(s["kones"], 1)

                dve.wait_ge(s["m_kw"], n * 16 + 16)
                dve.sem_inc(s["dve_at"], 1)
                dve.wait_ge(s["m_mb"], n + 1)
                dve.sem_inc(s["dve_at"], 1)

            def parts(i):
                key_parts(i, s["kv"], s["kch"])
                nc.vector.tensor_copy(vnext[:, :], b6[:, 2 * P:3 * P]).then_inc(s["vn"], 1)

            def mask_in_bf16(i):
                tile = dve.value_load(plan[0:1, bass.ds(i, 1)], min_val=0, max_val=T - 1)
                dve.wait_ge(s["mt"], i + 1)
                nc.vector.tensor_copy(mbf[:, :, :], mask_u8[:, :, bass.ds(tile * P, P)]).then_inc(s["mb"], 1)

            def mask_copy(i):
                dve.wait_ge(s["mt"], i + 2)
                nc.vector.tensor_copy(maskT[:, bass.ds(i % 2, 1), :], maskT_ps.rearrange("p (a q) -> p a q", a=1)).then_inc(s["mc"], 1)

            def value_copy():
                nc.vector.tensor_copy(vcur[:, :, 0:HD], vnext[:, :].rearrange("p (h d) -> p h d", d=HD)).then_inc(s["vc"], 1)

            def add(i, k):
                dve.wait_ge(s["pv"], i * 8 + k + 5)
                dve.wait_ge(s["ac"], i * 8 + k + 2)
                a = accU[:, k // 2, 512 * (k % 2):512 * (k % 2) + 512]
                nc.vector.tensor_tensor(a, bank[:, 4 + k % 2, :], a, ALU.add).then_inc(s["ac"], 1)

            dve.sem_inc(s["ac"], 1)
            mask_in_bf16(0)
            turned(0, s["ct"], s["ctsb"])
            parts(0)
            dve.wait_ge(s["vinit"], 1)
            dve.wait_ge(s["vn"], 1)
            value_copy()
            mask_copy(0)

            def tile_sums(i, masks):
                for k in range(8):
                    if k == 0 and masks:
                        mask_in_bf16(i + 1)
                    if k == 1:
                        turned(i + 1, s["ct"], s["ctsb"])
                    if k == 2:
                        dve.wait_ge(s["kw"], i * 16 + 16)
                        parts(i + 1)
                    if k >= 1:
                        add(i, k - 1)
                    if k == 5 and masks:
                        mask_copy(i + 1)
                add(i, 7)
                dve.wait_ge(s["vn"], i + 2)
                value_copy()

            partial = dve.value_load(plan[0:1, 66:67], min_val=0, max_val=T)
            with dve.If(partial):
                with dve.Fori(0, partial) as i:
                    tile_sums(i, True)
            with dve.If(n - partial):
                with dve.Fori(partial, n) as i:
                    tile_sums(i, False)
            dve.wait_ge(s["ac"], n * 8 + 2)
            dve.sem_inc(s["dve_at"], 1)

            dve.wait_ge(s["cs_ps"], 1)
            nc.vector.tensor_copy(csT[:, :], b6[:, 200:201]).then_inc(s["cs_sb"], 1)
            dve.wait_ge(s["cs_ps"], 2)
            nc.vector.tensor_copy(vsrow[:, :], b6[0:1, 256:384]).then_inc(s["cs_sb"], 1)
            dve.wait_ge(s["cs_ps"], 3)
            nc.vector.tensor_copy(vsumB[:, :], b6[:, 384:512]).then_inc(s["cs_sb"], 1)

            for hf in range(2):
                dve.wait_ge(s["u_ps"], hf + 1)
                U = bank[:, 4 * hf:4 * hf + 4, :].rearrange("p t (k c) -> p (t k) c", c=32)
                c0 = 5 * hf
                flag, weight, inv, tmp = (after[:, 5120 + 64 * k:5120 + 64 * k + (512 if k == 3 else 64)] for k in range(4))
                cq = ctxq[:, 4 * hf:4 * hf + 4, :].rearrange("p t (h c) -> p (t h) c", c=HD)
                tmp = tmp.rearrange("p (k c) -> p k c", c=HD)
                over = lambda a: a.rearrange("p (k a) -> p k a", a=1).broadcast_to([P, 64, HD])
                if hf:
                    dve.wait_ge(s["u_dve"], 5)
                nc.vector.tensor_scalar(flag, U[:, :, HD], 0.0, None, ALU.is_equal).then_inc(s["u_dve"], 1)
                dve.wait_ge(s["u_dve"], c0 + 1)
                nc.vector.scalar_tensor_tensor(weight, flag, float(S2), U[:, :, HD], ALU.mult, ALU.add).then_inc(s["u_dve"], 1)
                for t in range(4):
                    last = nc.vector.tensor_tensor(tmp[:, H * t:H * t + H, :], over(flag)[:, H * t:H * t + H, :],
                                                   vsumB[:, :].rearrange("p (h c) -> p h c", c=HD), ALU.mult)
                last.then_inc(s["u_dve"], 1)
                dve.wait_ge(s["u_dve"], c0 + 3)
                nc.vector.tensor_tensor(cq, tmp, U[:, :, 0:HD], ALU.add)
                nc.vector.reciprocal(inv, weight).then_inc(s["u_dve"], 1)
                dve.wait_ge(s["u_dve"], c0 + 4)
                nc.vector.tensor_tensor(cq, cq, over(inv), ALU.mult).then_inc(s["u_dve"], 1)
            for k in range(2):
                dve.wait_ge(s["cq_ps"], k + 1)
                nc.vector.tensor_copy(ctxqT[:, 512 * k:512 * k + 512], bank[:, k, :]).then_inc(s["cq_sb"], 1)
            dve.wait_ge(s["at_ps"], 1)
            nc.vector.tensor_tensor(x2, x_sb[:, :, :], bank[:, 2:4, :].rearrange("p a (t d) -> p (a t) d", d=D), ALU.add).then_inc(s["x2s"], 1)
            dve.wait_ge(s["x2s"], 1)
            layer_norm(dve, x2, xn2, sq2, s["ln2"], s["sqrt2"])
            for k in range(2):
                dve.wait_ge(s["x2T_ps"], k + 1)
                nc.vector.tensor_copy(x2T[:, 512 * k:512 * k + 512], bank[:, k, :]).then_inc(s["x2T_sb"], 1)

            c = [0]

            def step(ins):
                c[0] += 1
                ins.then_inc(s["gt"], 1)
                dve.wait_ge(s["gt"], c[0])

            dve.wait_ge(s["lg"], 1)
            ge = [g[:, k, :].rearrange("p (t e) -> p t e", e=E) for k in range(12)]
            ie = iota_e[:, :].rearrange("p (t e) -> p t e", e=E)
            b8 = lambda a: a.rearrange("p (t a) -> p t a", a=1).broadcast_to([P, QT, E])
            lg = bank[:, 2, 0:QT * E].rearrange("p (t e) -> p t e", e=E)
            step(nc.vector.tensor_reduce(g1[:, 0, :], lg, axis=AX.X, op=ALU.max))
            step(nc.vector.tensor_tensor(ge[0], lg, b8(g1[:, 0, :]), ALU.subtract))
            dve.wait_ge(s["gtexp"], 1)
            step(nc.vector.tensor_reduce(g1[:, 1, :], ge[1], axis=AX.X, op=ALU.add))
            step(nc.vector.reciprocal(g1[:, 2, :], g1[:, 1, :]))
            step(nc.vector.tensor_tensor(ge[2], ge[1], b8(g1[:, 2, :]), ALU.mult))
            cur = ge[2]
            for k in range(2):
                step(nc.vector.tensor_reduce(g1[:, 3, :], cur, axis=AX.X, op=ALU.max))
                step(nc.vector.tensor_tensor(ge[3], cur, b8(g1[:, 3, :]), ALU.is_lt))
                step(nc.vector.scalar_tensor_tensor(ge[4], ge[3], 64.0, ie, ALU.mult, ALU.add))
                step(nc.vector.tensor_reduce(g1[:, 4, :], ge[4], axis=AX.X, op=ALU.min))
                step(nc.vector.tensor_tensor(ge[5 + k], ie, b8(g1[:, 4, :]), ALU.is_equal))
                if k == 0:
                    step(nc.vector.scalar_tensor_tensor(ge[7], ge[5], -2.0, ge[2], ALU.mult, ALU.add))
                    cur = ge[7]
            step(nc.vector.tensor_tensor(ge[8], ge[5], ge[6], ALU.add))
            step(nc.vector.tensor_tensor(ge[9], ge[8], ge[2], ALU.mult))
            assert c[0] == GATE_STEPS
            for k in range(2):
                dve.wait_ge(s["gT_ps"], k + 1)
                nc.vector.tensor_copy(epi_e[:, 512 * k:512 * k + 512], bank[0:E, k, :]).then_inc(s["gT_sb"], 1)
            dve.wait_ge(s["b2ps"], 1)
            nc.vector.tensor_tensor(x2, x2, bank[:, 2:4, :].rearrange("p a (t d) -> p (a t) d", d=D), ALU.add).then_inc(s["yacc"], 1)
            for e in range(E):
                for t in range(QT):
                    dve.wait_ge(s["yps"], e * QT + t + 1)
                    dve.wait_ge(s["yacc"], max(1, (e - 1) * QT + t + 2))
                    last = nc.vector.scalar_tensor_tensor(x2[:, t, :], bank[:, 6 + t % 2, 0:P], ge[9][:, t, e:e + 1], x2[:, t, :],
                                                          ALU.mult, ALU.add).then_inc(s["yacc"], 1)

        @block.scalar
        def _(act):
            act.wait_ge(s["ln"], 6)
            nc.scalar.activation(stat[:, 2, :], stat[:, 1, :], ACT.Sqrt).then_inc(s["sqrt"], 1)
            act.wait_ge(s["wt_ps"], 1)
            nc.scalar.activation(wT[:, :, :], bank[:, 4, :].rearrange("p (a b) -> p a b", a=4), ACT.Copy).then_inc(s["wt_sb"], 1)
            act.wait_ge(s["wt_ps"], 2)
            nc.scalar.activation(gateT[:, :], bank[:, 5, 0:E], ACT.Copy).then_inc(s["wt_sb"], 1)
            nc.scalar.activation(b1T[:, :, :], bank[:, 5, 64:64 + FT * E].rearrange("p (a e) -> p a e", a=FT), ACT.Copy).then_inc(s["wt_sb"], 1)
            act.wait_ge(s["wt_sb"], 1)
            nc.scalar.activation(wk_turned[:, :].rearrange("p (d h) -> p h d", h=H), wT[:, 1, :].rearrange("p (h d) -> p h d", d=HD), ACT.Copy).then_inc(s["wk_sb"], 1)
            act.wait_ge(s["row_in"], 80)
            nc.scalar.activation(bk_turned[:, :].rearrange("p (d h) -> p h d", h=H), brow[0:1, 1, :].rearrange("p (h d) -> p h d", d=HD), ACT.Copy).then_inc(s["wk_sb"], 1)
            act.wait_ge(s["q_sb"], 2)
            act.wait_ge(s["row_in"], 80)
            for k in range(2):
                nc.scalar.activation(squares[:, k, :], bank[:, 2 + k, :], ACT.Square).then_inc(s["sqr"], 1)
            for c in range(CHUNKS + 1):
                if c < CHUNKS:
                    w = min(512, KW - 512 * c)
                    act.wait_ge(s["cc_ps"], c + 1)
                    nc.scalar.activation(ctx_cT[:, c % 2, 0:w], bank[:, c % 2, 0:w], ACT.Copy).then_inc(s["cc_sb"], 1)
                if c >= 1:
                    w = min(512, KW - 512 * (c - 1))
                    act.wait_ge(s["kk_ps"], c)
                    if c < 3:
                        act.wait_ge(s["qn_ps"], 1)
                    else:
                        act.wait_ge(s["kn_ps"], c - 2)
                    nc.scalar.activation(squares[:, (c - 1) % 2, 0:w], bank[:, 6 + (c - 1) % 2, 0:w], ACT.Square, bias=bkcol[:, :]).then_inc(s["sqr"], 1)
            act.wait_ge(s["bd"], 5)
            nc.scalar.activation(bound[:, 1:2], bound[:, 0:1], ACT.Sqrt, scale=1.02).then_inc(s["bd_sqrt"], 1)
            act.wait_ge(s["plan_ready"], 1)
            n = act.value_load(plan[0:1, 64:65], min_val=1, max_val=T)
            act.sem_inc(s["ex"], 2)
            with act.Fori(0, n) as i:
                for u in range(16):
                    act.wait_ge(s["qk"], i * 16 + u + 18)
                    act.wait_ge(s["pv"], i * 8 + u // 2 + 1)
                    nc.scalar.activation(probs[u % 8], bank[:, 2 * (u % 2):2 * (u % 2) + 2, :].rearrange("p a b -> p (a b)"),
                                         ACT.Exp, scale=SCALE).then_inc(s["ex"], 1)
            for k in range(16):
                act.wait_ge(s["wtb_ps"], k + 1)
                dst = w1T[:, k % 8, :, :] if k < 8 else w2T[:, k - 8, :, :]
                nc.scalar.activation(dst, bank[:, (2 if k < 8 else 6) + k % 2, :].rearrange("p (a b) -> p a b", a=FT), ACT.Copy).then_inc(s["wtb_sb"], 1)
                if k == 12:
                    act.wait_ge(s["ln2"], 6)
                    nc.scalar.activation(stat[:, 2, :], stat[:, 1, :], ACT.Sqrt).then_inc(s["sqrt2"], 1)
            act.wait_ge(s["gt"], 2)
            nc.scalar.activation(g[:, 1, :], g[:, 0, :], ACT.Exp).then_inc(s["gtexp"], 1)
            for e in range(E):
                for k in range(2 * FT):
                    c = e * 2 * FT + k
                    act.wait_ge(s["hps"], c + 1)
                    if e >= 2 and k == 0:
                        act.wait_ge(s["yps"], (e - 1) * QT)
                    nc.scalar.activation(hT[:, e % 2, k // 2, 512 * (k % 2):512 * (k % 2) + 512], bank[:, 4 + c % 2, :],
                                         ACT.Gelu_apprx_tanh, bias=b1T[:, k // 2, e:e + 1]).then_inc(s["hact"], 1)

        @block.tensor
        def _(pe):
            mm = nc.tensor.matmul
            pe.wait_ge(s["const"], 11)
            pe.wait_ge(s["w_in"], 64)
            for i in range(4):
                last = nc.tensor.transpose(bank[:, 4, i * P:(i + 1) * P], wraw[:, i, :], ident[:, :])
            last.then_inc(s["wt_ps"], 1)
            pe.wait_ge(s["ln"], 12)
            for t in range(QT):
                last = nc.tensor.transpose(bank[:, t // 4, (t % 4) * P:(t % 4 + 1) * P], xn[:, t, :], ident[:, :])
                if t % 4 == 3:
                    last.then_inc(s["xnT_ps"], 1)
            pe.wait_ge(s["wt_sb"], 1)
            pe.wait_ge(s["row_in"], 80)
            for k in range(2):
                pe.wait_ge(s["xT_sb"], k + 1)
                mm(bank[:, 2 + k, :], wT[:, 0, :], xT[:, 512 * k:512 * k + 512], start=True, stop=False)
                last = mm(bank[:, 2 + k, :], brow[0:1, 0, :], ones[0:1, :], start=False, stop=True)
            last.then_inc(s["q_ps"], 1)
            pe.wait_ge(s["gate_in"], 16)
            pe.wait_ge(s["b1_in"], 16)
            last = nc.tensor.transpose(bank[:, 5, 0:E], gate_raw[:, :], ident[0:E, 0:E])
            for a in range(FT):
                last = nc.tensor.transpose(bank[:, 5, 64 + a * E:64 + (a + 1) * E], b1_raw[:, a * P:(a + 1) * P], ident[0:E, 0:E])
            last.then_inc(s["wt_ps"], 1)
            pe.wait_ge(s["wt_sb"], 3)
            pe.wait_ge(s["hs"], 1)
            for k in range(2):
                pe.wait_ge(s["sqr"], k + 1)
                for t in range(4):
                    last = mm(sizes[:, T + 4 * k + t, :], squares[:, k, t * P:(t + 1) * P], headsel[:, :], start=True, stop=True)
            last.then_inc(s["qn_ps"], 1)
            pe.wait_ge(s["q_sb"], 4)
            pe.wait_ge(s["ctx_in"], 16)
            cuts = {t0: k for k, (t0, _) in enumerate(CTX_CUTS)}
            for c in range(CHUNKS + 2):
                if c < CHUNKS:
                    tiles = range(4 * c, min(4 * c + 4, T))
                    if c >= 2:
                        pe.wait_ge(s["cc_sb"], c - 1)
                    for t in tiles:
                        if t in cuts:
                            pe.wait_ge(ctx_in_s[cuts[t]], 16)
                        last = nc.tensor.transpose(bank[:, c % 2, (t - 4 * c) * P:(t - 4 * c + 1) * P], ctx_sb[:, t, :], ident[:, :])
                    last.then_inc(s["cc_ps"], 1)
                if 1 <= c <= CHUNKS:
                    w = min(512, KW - 512 * (c - 1))
                    pe.wait_ge(s["cc_sb"], c)
                    if c >= 3:
                        pe.wait_ge(s["sqr"], c)
                    mm(bank[:, 6 + (c - 1) % 2, 0:w], wT[:, 1, :], ctx_cT[:, (c - 1) % 2, 0:w], start=True, stop=True).then_inc(s["kk_ps"], 1)
                if c >= 2:
                    w = min(512, KW - 512 * (c - 2))
                    pe.wait_ge(s["sqr"], c + 1)
                    for t in range(w // P):
                        last = mm(sizes[:, 4 * (c - 2) + t, :], squares[:, (c - 2) % 2, t * P:(t + 1) * P], headsel[:, :], start=True, stop=True)
                    last.then_inc(s["kn_ps"], 1)
            pe.wait_ge(s["sqr"], CHUNKS + 2)
            pe.wait_ge(s["pl_sb"], 1)
            mm(b6[0:T, 0:1], cnt4[:, 0, :], ones[:, 0:1], start=True, stop=True)
            mm(b6[0:T, 1:2], cnt4[:, 1, :], ones[:, 0:1], start=True, stop=True).then_inc(s["pl_ps"], 1)
            pe.wait_ge(s["bd"], 2)
            nc.tensor.transpose(bank[0:H, 2, 0:P], nmax[:, 0, :], ident[:, :])
            nc.tensor.transpose(bank[0:H, 2, P:2 * P], nmax[:, 1, :], ident[:, :]).then_inc(s["bd_ps"], 1)
            pe.wait_ge(s["pl_sb"], 3)
            mm(b6[0:T, 3:4], tri[0:T, 0:T], tcol[0:T, 2:3], start=True, stop=True)
            mm(b6[0:T, 4:5], tri[0:T, 0:T], tcol[0:T, 1:2], start=True, stop=False)
            mm(b6[0:T, 4:5], ones[0:T, 0:T], tcol[0:T, 2:3], start=False, stop=True).then_inc(s["pl_ps"], 1)
            pe.wait_ge(s["bd"], 4)
            mm(bank[0:1, 4, 0:H], norms[:, 2:3], ident[0:H, 0:H], start=True, stop=True).then_inc(s["bd_ps"], 1)
            pe.wait_ge(s["pl_sb"], 6)
            mm(b6[0:1, 64:128], iota_p[0:T, :], hot[0:T, :], start=True, stop=True)
            mm(b6[0:1, 128:129], tcol[0:T, 0:1], ones[0:T, 0:1], start=True, stop=True)
            mm(b6[0:1, 129:130], tcol[0:T, 2:3], ones[0:T, 0:1], start=True, stop=True).then_inc(s["pl_ps"], 1)
            pe.wait_ge(s["plan_ready"], 1)
            mm(bank[:, 4, 64:65], ones[0:1, 0:P], bound[0:1, 3:4], start=True, stop=True).then_inc(s["bd_row"], 1)
            pe.wait_ge(s["pl_sb"], 7)
            n = pe.value_load(plan[0:1, 64:65], min_val=1, max_val=T)

            def turn(i, cb, ct):
                pe.wait_ge(cb, i + 1)
                nc.tensor.transpose(b6[:, 0:P], cbuf[:, :], ident[:, :]).then_inc(ct, 1)

            def project(i, ctsb, kv, values):
                pe.wait_ge(ctsb, i + 1)
                mm(b6[:, P:2 * P], wk_turned[:, :], cT[:, :], start=True, stop=False)
                last = mm(b6[:, P:2 * P], bk_turned[:, :], ones[0:1, 0:P], start=False, stop=True)
                if values:
                    mm(b6[:, 2 * P:3 * P], cT[:, :], wT[:, 2, :], start=True, stop=False)
                    last = mm(b6[:, 2 * P:3 * P], ones[0:1, 0:P], brow[0:1, 2, :], start=False, stop=True)
                last.then_inc(kv, 1)

            pe.wait_ge(s["wk_sb"], 2)
            pe.wait_ge(s["qr"], 16 * NC)
            pe.wait_ge(s["kshift"], 16)
            general = pe.value_load(plan[0:1, 65:66], min_val=0, max_val=1)
            with pe.If(general):
                pe.sem_inc(s["m_ct"], 1)
                pe.sem_inc(s["m_qk"], 16)
                pe.sem_inc(s["m_qk"], 1)
                turn(0, s["m_cb"], s["m_ct"])
                project(0, s["m_ctsb"], s["m_kv"], False)
                with pe.Fori(0, n) as i:
                    pe.wait_ge(s["m_kr"], i * 48 + 48)
                    pe.wait_ge(s["m_mb"], i + 1)
                    for u in range(16):
                        t, hh = u // 2, u % 2
                        pe.wait_ge(s["m_red"], i * 16 + u + 1)
                        for a in range(2):
                            o = bank[:, 2 * hh + a, :]
                            mm(o, nbig[:, :], mbf[:, t, :].rearrange("p (a k) -> p a k", a=1).broadcast_to([P, 4, P]), start=True, stop=False)
                            for b in range(4):
                                h = 8 * hh + 4 * a + b
                                last = mm(o[:, b * P:(b + 1) * P], qS[:, h, t * P:(t + 1) * P], keys[:, bass.ds(i % 2, 1), h, :].rearrange("p a k -> p (a k)"), start=False, stop=(b == 3))
                        last.then_inc(s["m_qk"], 1)
                        if u == 3:
                            pe.wait_ge(s["m_kch"], i * 4 + 4)
                            turn(i + 1, s["m_cb"], s["m_ct"])
                            project(i + 1, s["m_ctsb"], s["m_kv"], False)
                pe.wait_ge(s["m_fin"], 5)
                pt = bank[:, 0, 0:192].bitcast(BF16)
                for c in range(3):
                    last = nc.tensor.transpose(pt[:, c * P:(c + 1) * P], mparts[:, c, :], identb[:, :])
                last.then_inc(s["m_finT"], 1)
                pe.wait_ge(s["m_kch"], n * 4 + 4)

                pe.wait_ge(s["shift"], 48)
                pe.wait_ge(s["kones"], 1)
                pe.sem_inc(s["pe_at"], 1)
            pe.sem_inc(s["ct"], 1)
            pe.sem_inc(s["pv"], 4)
            pe.sem_inc(s["qk"], 16)
            pe.sem_inc(s["qk"], 1)
            pe.sem_inc(s["mt"], 1)

            def scores(i, u, ui, tile, hides):
                pe.wait_ge(s["ex"], i * 16 + ui + 1)
                kk = u // 2
                for a in range(2):
                    h = 4 * (kk // 2) + 2 * (u % 2) + a
                    o, cols = bank[:, 2 * (u % 2) + a, :], slice(512 * (kk % 2), 512 * (kk % 2) + 512)
                    if hides:
                        mm(o, nbig[:, :], maskT[:, bass.ds(tile % 2, 1), cols].rearrange("p a q -> p (a q)"), start=True, stop=False)
                    last = mm(o, keys[:, bass.ds(tile % 2, 1), h, :].rearrange("p a k -> p (a k)"), qS[:, h, cols], start=not hides, stop=True)
                last.then_inc(s["qk"], 1)

            def values(i, k, half):
                if half == 0:
                    pe.wait_ge(s["ex"], i * 16 + 2 * k + 4)
                    pe.wait_ge(s["ac"], i * 8 + k + 1)
                if half == 0 and k == 0:
                    pe.wait_ge(s["vc"], i + 1)
                for j in range(4):
                    q = 512 * (j % 2) + 256 * half
                    last = mm(bank[32 * j:32 * j + 32, 4 + k % 2, 256 * half:256 * half + 256], vcur[:, 4 * (k // 2) + j, :],
                              probs[(2 * k + j // 2) % 8][:, q:q + 256], start=True, stop=True, tile_position=(0, 32 * j))
                if half == 1:
                    last.then_inc(s["pv"], 1)

            def mask_turn(i):
                pe.wait_ge(s["mb"], i + 1)
                for t in range(QT):
                    last = nc.tensor.transpose(maskT_ps[:, t * P:(t + 1) * P], mbf[:, t, :], identb[:, :])
                last.then_inc(s["mt"], 1)

            turn(0, s["cb"], s["ct"])
            project(0, s["ctsb"], s["kv"], True)
            mask_turn(0)
            pe.wait_ge(s["kr"], 48)
            pe.wait_ge(s["mc"], 1)
            scores(0, 0, 0, 0, True)
            scores(0, 1, 1, 0, True)

            def tile_steps(i, hides):
                for k in range(8):
                    if k == 7:
                        pe.wait_ge(s["kr"], i * 48 + 96)
                        if hides:
                            pe.wait_ge(s["mc"], i + 2)
                    scores(i, (2 * k + 2) % 16, 2 * k + 2, i + (k == 7), hides)
                    if k >= 1:
                        values(i, k - 1, 1)
                    scores(i, (2 * k + 3) % 16, 2 * k + 3, i + (k == 7), hides)
                    values(i, k, 0)
                    if k == 7:
                        values(i, k, 1)
                    if k == 0:
                        pe.wait_ge(s["vn"], i + 1)
                        turn(i + 1, s["cb"], s["ct"])
                    if k == 1:
                        project(i + 1, s["ctsb"], s["kv"], True)
                    if k == 3 and hides:
                        mask_turn(i + 1)

            partial = pe.value_load(plan[0:1, 66:67], min_val=0, max_val=T)
            with pe.If(partial):
                with pe.Fori(0, partial) as i:
                    tile_steps(i, True)
            with pe.If(n - partial):
                with pe.Fori(partial, n) as i:
                    tile_steps(i, False)

            def sums_turn(half):
                for t in range(4 * half, 4 * half + 4):
                    for gg in range(4):
                        last = nc.tensor.transpose(bank[:, t, gg * P:(gg + 1) * P], accU[:, gg, t * P:(t + 1) * P], ident[:, :])
                last.then_inc(s["u_ps"], 1)

            pe.wait_ge(s["ac"], n * 8 + 2)
            pe.wait_ge(s["vc"], n + 1)
            sums_turn(0)
            pe.wait_ge(s["fold"], FOLD_STEPS)
            pe.wait_ge(s["s2"], 1)
            mm(b6[:, 200:201], csum[:, :], ones[:, 0:1], start=True, stop=True).then_inc(s["cs_ps"], 1)
            pe.wait_ge(s["cs_sb"], 1)
            mm(b6[0:1, 256:384], csT[:, :], wT[:, 2, :], start=True, stop=True).then_inc(s["cs_ps"], 1)
            pe.wait_ge(s["cs_sb"], 2)
            mm(b6[:, 384:512], ones[0:1, 0:P], vsrow[0:1, :], start=True, stop=False)
            mm(b6[:, 384:512], s2row[0:1, :], brow[0:1, 2, :], start=False, stop=True).then_inc(s["cs_ps"], 1)
            pe.wait_ge(s["cs_sb"], 3)

            sums_turn(1)
            def expert_weights(k0, k1):
                pe.wait_ge(s["w1_in" if k0 < E else "w2_in"], 16)
                for k in range(k0, k1):
                    if k >= 2:
                        pe.wait_ge(s["wtb_sb"], k - 1)
                    for a in range(FT):
                        src = w1raw[:, a, k, :] if k < E else w2raw[:, k - E, a * P:(a + 1) * P]
                        last = nc.tensor.transpose(bank[:, (2 if k < E else 6) + k % 2, a * P:(a + 1) * P], src, ident[:, :])
                    last.then_inc(s["wtb_ps"], 1)

            for hf in range(2):
                pe.wait_ge(s["u_dve"], 5 * hf + 5)
                for t in range(4 * hf, 4 * hf + 4):
                    last = nc.tensor.transpose(bank[:, t // 4, (t % 4) * P:(t % 4 + 1) * P], ctxq[:, t, :], ident[:, :])
                last.then_inc(s["cq_ps"], 1)
                if hf == 0:
                    expert_weights(0, E)
            pe.wait_ge(s["wtb_sb"], E)
            for t in range(QT):
                pe.wait_ge(s["cq_sb"], t // 4 + 1)
                o = bank[:, 2 + t // 4, (t % 4) * P:(t % 4 + 1) * P]
                mm(o, ctxqT[:, t * P:(t + 1) * P], wT[:, 3, :], start=True, stop=False)
                last = mm(o, ones[0:1, 0:P], brow[0:1, 3, :], start=False, stop=True)
            last.then_inc(s["at_ps"], 1)
            expert_weights(E, 2 * E)
            pe.wait_ge(s["ln2"], 12)
            for t in range(QT):
                last = nc.tensor.transpose(bank[:, t // 4, (t % 4) * P:(t % 4 + 1) * P], xn2[:, t, :], ident[:, :])
                if t % 4 == 3:
                    last.then_inc(s["x2T_ps"], 1)
            pe.wait_ge(s["x2T_sb"], 2)
            for t in range(QT):
                last = mm(bank[:, 2, t * E:(t + 1) * E], x2T[:, t * P:(t + 1) * P], gateT[:, :], start=True, stop=True)
            last.then_inc(s["lg"], 1)

            def up(e):
                for k in range(2 * FT):
                    c = e * 2 * FT + k
                    if c >= 2:
                        pe.wait_ge(s["hact"], c - 1)
                    mm(bank[:, 4 + c % 2, :], w1T[:, e, k // 2, :], x2T[:, 512 * (k % 2):512 * (k % 2) + 512],
                       start=True, stop=True).then_inc(s["hps"], 1)

            def down(e):
                pe.wait_ge(s["hact"], (e + 1) * 2 * FT)
                for t in range(QT):
                    c = e * QT + t
                    if c >= 2:
                        pe.wait_ge(s["yacc"], c)
                    for a in range(FT):
                        last = mm(bank[:, 6 + t % 2, 0:P], hT[:, e % 2, a, t * P:(t + 1) * P], w2T[:, e, a, :],
                                  start=(a == 0), stop=(a == FT - 1))
                    last.then_inc(s["yps"], 1)

            up(0)
            pe.wait_ge(s["gt"], GATE_STEPS)
            pe.wait_ge(s["b2_in"], 16)
            for t in range(QT):
                last = nc.tensor.transpose(bank[0:E, t // 4, (t % 4) * P:(t % 4 + 1) * P], g[:, 9, t * E:(t + 1) * E], ident[:, :])
                if t % 4 == 3:
                    last.then_inc(s["gT_ps"], 1)
            pe.wait_ge(s["gT_sb"], 2)
            for t in range(QT):
                last = mm(bank[:, 2 + t // 4, (t % 4) * P:(t % 4 + 1) * P], epi_e[:, t * P:(t + 1) * P], b2_sb[:, :], start=True, stop=True)
            last.then_inc(s["b2ps"], 1)
            for e in range(E):
                if e + 1 < E:
                    up(e + 1)
                down(e)


_INS = ['x', 'ctx_1024', 'mask_BxSxS2_bk1', 'L0_xattn_Wq', 'L0_xattn_bq', 'L0_xattn_Wk', 'L0_xattn_bk', 'L0_xattn_Wv',
        'L0_xattn_bv', 'L0_xattn_Wo', 'L0_xattn_bo', 'L0_ffn_gate_w', 'L0_ffn_w1', 'L0_ffn_b1', 'L0_ffn_w2', 'L0_ffn_b2']


def kernel(**inputs):
    import numpy as _np
    import concourse.bacc as _bacc
    from concourse import mybir as _mybir
    from concourse.bass_utils import run_bass_kernel_spmd as _run

    nc = _bacc.Bacc("TRN2", target_bir_lowering=False, num_devices=1)
    arrays, args = {}, []
    for name in _INS:
        a = _np.ascontiguousarray(inputs[name])
        arrays[f"in_{name}_dram"] = a
        args.append(nc.dram_tensor(f"in_{name}_dram", a.shape, _mybir.dt.from_np(a.dtype), kind="ExternalInput").ap())
    args.append(nc.dram_tensor("out_0_dram", (1, S, D), F32, kind="ExternalOutput").ap())
    build(nc, *args)
    r = _run(nc, [arrays], core_ids=[0])
    return r.results[0]["out_0_dram"]
```
